# Optimizing a Trainium2 kernel written in Bass

```python
import numpy as np
import jax
import jax.numpy as jnp

def _softmax(x, axis=-1):
    return jax.nn.softmax(x, axis=axis)

def _gelu(x):
    return jax.nn.gelu(x, approximate=True)

def _silu(x):
    return jax.nn.silu(x)

def _sigmoid(x):
    return jax.nn.sigmoid(x)

def _layernorm(x, axis=-1, eps=1e-05):
    m = jnp.mean(x, axis=axis, keepdims=True)
    v = jnp.var(x, axis=axis, keepdims=True)
    return (x - m) / jnp.sqrt(v + eps)

def _scatter_add(tgt, idx, src, axis=0):
    return tgt.at[idx].add(src)

def _segment_sum(src, seg, n):
    return jax.ops.segment_sum(src, seg, n)
kernel_name = 'mk_vit_tower_d1_tok_img768_r4_a7be16'

def setup_inputs(seed: int=0):
    np.random.seed(seed)
    _w = jnp.asarray

    def _rec_inputs():
        import jax
        import jax.numpy as jnp
        _rk = jax.random.key(seed)
        x = -0.00016672 + 0.999947 * jax.random.normal(jax.random.fold_in(_rk, 1), (64, 3, 224, 224), jnp.float32)
        return x
    x = _rec_inputs()

    def _L0_tok_setup():
        import jax, jax.numpy as jnp
        import numpy as np
        P1 = 16
        P2 = 16
        C = 3
        PATCH_DIM = P1 * P2 * C
        OUT_DIM = 192
        EPS = 1e-05

        def _layernorm(x, gamma, beta):
            mu = jnp.mean(x, axis=-1, keepdims=True)
            var = jnp.var(x, axis=-1, keepdims=True)
            return (x - mu) * jax.lax.rsqrt(var + EPS) * gamma + beta
        key = jax.random.key(seed)
        k1, k2 = jax.random.split(key)
        features = jax.random.normal(k1, (64, C, 96, 96), dtype=jnp.float32)
        ln1_g = jnp.ones((PATCH_DIM,), jnp.float32)
        ln1_b = jnp.zeros((PATCH_DIM,), jnp.float32)
        W = jax.random.normal(k2, (PATCH_DIM, OUT_DIM), dtype=jnp.float32) * (1.0 / np.sqrt(PATCH_DIM))
        b = jnp.zeros((OUT_DIM,), jnp.float32)
        ln2_g = jnp.ones((OUT_DIM,), jnp.float32)
        ln2_b = jnp.zeros((OUT_DIM,), jnp.float32)
        return {'features': features, 'ln1_g': ln1_g, 'ln1_b': ln1_b, 'W': W, 'b': b, 'ln2_g': ln2_g, 'ln2_b': ln2_b}
    _L0_tok_all = _L0_tok_setup()
    _L0_tok_in = {k: v for k, v in _L0_tok_all.items() if k in ('ln1_g', 'ln1_b', 'W', 'b', 'ln2_g', 'ln2_b')}
    del _L0_tok_all

    def _L0_attn_setup():
        import jax, jax.numpy as jnp
        import numpy as np
        DIM = 192
        HEADS = 12
        HEAD_DIM = DIM // HEADS
        SCALE = HEAD_DIM ** (-0.5)
        key = jax.random.key(seed)
        k_x, k_wqkv, k_bqkv, k_wp, k_bp = jax.random.split(key, 5)
        B, P = (4, 512)
        x = jax.random.normal(k_x, (B, P, DIM), dtype=jnp.float32)
        w_qkv = jax.random.normal(k_wqkv, (3 * DIM, DIM), dtype=jnp.float32) * DIM ** (-0.5)
        b_qkv = jax.random.normal(k_bqkv, (3 * DIM,), dtype=jnp.float32) * 0.02
        w_proj = jax.random.normal(k_wp, (DIM, DIM), dtype=jnp.float32) * DIM ** (-0.5)
        b_proj = jax.random.normal(k_bp, (DIM,), dtype=jnp.float32) * 0.02
        return {'x': x, 'w_qkv': w_qkv, 'b_qkv': b_qkv, 'w_proj': w_proj, 'b_proj': b_proj}
    _L0_attn_all = _L0_attn_setup()
    _L0_attn_in = {k: v for k, v in _L0_attn_all.items() if k in ('w_qkv', 'b_qkv', 'w_proj', 'b_proj')}
    del _L0_attn_all

    def _L0_ffn_setup():
        import jax, jax.numpy as jnp
        import numpy as np
        E = 192
        H = 12
        D = E // H
        HID = 768
        NEXP = 4
        TOPK = 2
        EPS = 1e-05

        def _ln(x, g, b):
            m = jnp.mean(x, axis=-1, keepdims=True)
            v = jnp.mean(jnp.square(x - m), axis=-1, keepdims=True)
            return (x - m) * jax.lax.rsqrt(v + EPS) * g + b
        key = jax.random.key(seed)
        ks = jax.random.split(key, 10)
        s = 0.02
        return {'x': jax.random.normal(ks[0], (8, 256, E), jnp.float32), 'ln1_g': jnp.ones((E,), jnp.float32), 'ln1_b': jnp.zeros((E,), jnp.float32), 'in_w': jax.random.normal(ks[1], (3 * E, E), jnp.float32) * s, 'in_b': jnp.zeros((3 * E,), jnp.float32), 'out_w': jax.random.normal(ks[2], (E, E), jnp.float32) * s, 'out_b': jnp.zeros((E,), jnp.float32), 'mlp_w1': jax.random.normal(ks[3], (E, HID), jnp.float32) * s, 'mlp_b1': jnp.zeros((HID,), jnp.float32), 'mlp_w2': jax.random.normal(ks[4], (HID, E), jnp.float32) * s, 'mlp_b2': jnp.zeros((E,), jnp.float32), 'ln2_g': jnp.ones((E,), jnp.float32), 'ln2_b': jnp.zeros((E,), jnp.float32), 'gate_w': jax.random.normal(ks[5], (NEXP, E), jnp.float32) * s, 'gate_b': jnp.zeros((NEXP,), jnp.float32), 'exp_w1': jax.random.normal(ks[6], (NEXP, E, HID), jnp.float32) * s, 'exp_b1': jnp.zeros((NEXP, HID), jnp.float32), 'exp_w2': jax.random.normal(ks[7], (NEXP, HID, E), jnp.float32) * s, 'exp_b2': jnp.zeros((NEXP, E), jnp.float32)}
    _L0_ffn_all = _L0_ffn_setup()
    _L0_ffn_in = {k: v for k, v in _L0_ffn_all.items() if k in ('ln1_g', 'ln1_b', 'in_w', 'in_b', 'out_w', 'out_b', 'mlp_w1', 'mlp_b1', 'mlp_w2', 'mlp_b2', 'ln2_g', 'ln2_b', 'gate_w', 'gate_b', 'exp_w1', 'exp_b1', 'exp_w2', 'exp_b2')}
    del _L0_ffn_all
    return {'x': x, 'L0_tok_ln1_g': _L0_tok_in['ln1_g'], 'L0_tok_ln1_b': _L0_tok_in['ln1_b'], 'L0_tok_W': _L0_tok_in['W'], 'L0_tok_b': _L0_tok_in['b'], 'L0_tok_ln2_g': _L0_tok_in['ln2_g'], 'L0_tok_ln2_b': _L0_tok_in['ln2_b'], 'L0_attn_w_qkv': _L0_attn_in['w_qkv'], 'L0_attn_b_qkv': _L0_attn_in['b_qkv'], 'L0_attn_w_proj': _L0_attn_in['w_proj'], 'L0_attn_b_proj': _L0_attn_in['b_proj'], 'L0_ffn_ln1_g': _L0_ffn_in['ln1_g'], 'L0_ffn_ln1_b': _L0_ffn_in['ln1_b'], 'L0_ffn_in_w': _L0_ffn_in['in_w'], 'L0_ffn_in_b': _L0_ffn_in['in_b'], 'L0_ffn_out_w': _L0_ffn_in['out_w'], 'L0_ffn_out_b': _L0_ffn_in['out_b'], 'L0_ffn_mlp_w1': _L0_ffn_in['mlp_w1'], 'L0_ffn_mlp_b1': _L0_ffn_in['mlp_b1'], 'L0_ffn_mlp_w2': _L0_ffn_in['mlp_w2'], 'L0_ffn_mlp_b2': _L0_ffn_in['mlp_b2'], 'L0_ffn_ln2_g': _L0_ffn_in['ln2_g'], 'L0_ffn_ln2_b': _L0_ffn_in['ln2_b'], 'L0_ffn_gate_w': _L0_ffn_in['gate_w'], 'L0_ffn_gate_b': _L0_ffn_in['gate_b'], 'L0_ffn_exp_w1': _L0_ffn_in['exp_w1'], 'L0_ffn_exp_b1': _L0_ffn_in['exp_b1'], 'L0_ffn_exp_w2': _L0_ffn_in['exp_w2'], 'L0_ffn_exp_b2': _L0_ffn_in['exp_b2']}

def reference(x, L0_tok_ln1_g, L0_tok_ln1_b, L0_tok_W, L0_tok_b, L0_tok_ln2_g, L0_tok_ln2_b, L0_attn_w_qkv, L0_attn_b_qkv, L0_attn_w_proj, L0_attn_b_proj, L0_ffn_ln1_g, L0_ffn_ln1_b, L0_ffn_in_w, L0_ffn_in_b, L0_ffn_out_w, L0_ffn_out_b, L0_ffn_mlp_w1, L0_ffn_mlp_b1, L0_ffn_mlp_w2, L0_ffn_mlp_b2, L0_ffn_ln2_g, L0_ffn_ln2_b, L0_ffn_gate_w, L0_ffn_gate_b, L0_ffn_exp_w1, L0_ffn_exp_b1, L0_ffn_exp_w2, L0_ffn_exp_b2):
    import jax
    import jax.numpy as jnp

    def _L0_tok_ref(features, ln1_g, ln1_b, W, b, ln2_g, ln2_b):
        import jax, jax.numpy as jnp
        import numpy as np
        P1 = 16
        P2 = 16
        C = 3
        PATCH_DIM = P1 * P2 * C
        OUT_DIM = 192
        EPS = 1e-05

        def _layernorm(x, gamma, beta):
            mu = jnp.mean(x, axis=-1, keepdims=True)
            var = jnp.var(x, axis=-1, keepdims=True)
            return (x - mu) * jax.lax.rsqrt(var + EPS) * gamma + beta
        B, c, H, Wd = features.shape
        h, w = (H // P1, Wd // P2)
        x = features.reshape(B, c, h, P1, w, P2)
        x = jnp.transpose(x, (0, 2, 4, 3, 5, 1))
        x = x.reshape(B, h * w, P1 * P2 * c)
        x = _layernorm(x, ln1_g, ln1_b)
        x = jnp.einsum('bnd,de->bne', x, W) + b
        x = _layernorm(x, ln2_g, ln2_b)
        return x

    def _L0_attn_ref(x, w_qkv, b_qkv, w_proj, b_proj):
        import jax, jax.numpy as jnp
        import numpy as np
        DIM = 192
        HEADS = 12
        HEAD_DIM = DIM // HEADS
        SCALE = HEAD_DIM ** (-0.5)
        B, P, D = x.shape
        qkv = x @ w_qkv.T + b_qkv
        qkv = qkv.reshape(B, P, 3, HEAD_DIM, HEADS)
        qkv = jnp.transpose(qkv, (2, 0, 4, 1, 3))
        q, k, v = (qkv[0], qkv[1], qkv[2])
        atten = jnp.einsum('bhqd,bhkd->bhqk', q, k) * SCALE
        atten = jax.nn.softmax(atten, axis=-1)
        out = jnp.einsum('bhqk,bhkd->bhqd', atten, v)
        out = jnp.transpose(out, (0, 2, 1, 3)).reshape(B, P, D)
        return out @ w_proj.T + b_proj

    def _L0_ffn_ref(x, ln1_g, ln1_b, in_w, in_b, out_w, out_b, mlp_w1, mlp_b1, mlp_w2, mlp_b2, ln2_g, ln2_b, gate_w, gate_b, exp_w1, exp_b1, exp_w2, exp_b2):
        import jax, jax.numpy as jnp
        import numpy as np
        E = 192
        H = 12
        D = E // H
        HID = 768
        NEXP = 4
        TOPK = 2
        EPS = 1e-05

        def _ln(x, g, b):
            m = jnp.mean(x, axis=-1, keepdims=True)
            v = jnp.mean(jnp.square(x - m), axis=-1, keepdims=True)
            return (x - m) * jax.lax.rsqrt(v + EPS) * g + b
        B, N, _ = x.shape
        h = _ln(x, ln1_g, ln1_b)
        qkv = h @ in_w.T + in_b
        q, k, v = jnp.split(qkv, 3, axis=-1)
        q = q.reshape(B, N, H, D)
        k = k.reshape(B, N, H, D)
        v = v.reshape(B, N, H, D)
        scores = jnp.einsum('bqhd,bkhd->bhqk', q, k) / jnp.sqrt(jnp.float32(D))
        attn = jax.nn.softmax(scores, axis=-1)
        ctx = jnp.einsum('bhqk,bkhd->bqhd', attn, v).reshape(B, N, E)
        x = x + ctx @ out_w.T + out_b
        x = x + jax.nn.gelu(x @ mlp_w1 + mlp_b1, approximate=False) @ mlp_w2 + mlp_b2
        xm = _ln(x, ln2_g, ln2_b)
        logits = xm @ gate_w.T + gate_b
        topv, topi = jax.lax.top_k(logits, TOPK)
        gates = jax.nn.softmax(topv, axis=-1)
        onehot = jax.nn.one_hot(topi, NEXP, dtype=x.dtype)
        comb = jnp.einsum('bnk,bnke->bne', gates, onehot)
        moe_out = jnp.zeros_like(x)
        for e in range(NEXP):
            he = jax.nn.gelu(xm @ exp_w1[e] + exp_b1[e], approximate=False)
            oe = he @ exp_w2[e] + exp_b2[e]
            moe_out = moe_out + comb[..., e:e + 1] * oe
        return x + moe_out
    h = _L0_tok_ref(x, L0_tok_ln1_g, L0_tok_ln1_b, L0_tok_W, L0_tok_b, L0_tok_ln2_g, L0_tok_ln2_b)
    h = h + _L0_attn_ref(_layernorm(h, axis=-1), L0_attn_w_qkv, L0_attn_b_qkv, L0_attn_w_proj, L0_attn_b_proj)
    h = h + _L0_ffn_ref(_layernorm(h, axis=-1), L0_ffn_ln1_g, L0_ffn_ln1_b, L0_ffn_in_w, L0_ffn_in_b, L0_ffn_out_w, L0_ffn_out_b, L0_ffn_mlp_w1, L0_ffn_mlp_b1, L0_ffn_mlp_w2, L0_ffn_mlp_b2, L0_ffn_ln2_g, L0_ffn_ln2_b, L0_ffn_gate_w, L0_ffn_gate_b, L0_ffn_exp_w1, L0_ffn_exp_b1, L0_ffn_exp_w2, L0_ffn_exp_b2)
    return h

_drawn_inputs = setup_inputs


def setup_inputs(seed=0):
    import zlib

    import numpy as np

    out = dict(_drawn_inputs(seed))
    spreads = {'L0_tok_ln1_g': (1.0, 0.2),
     'L0_tok_ln1_b': (0.0, 0.1),
     'L0_tok_b': (0.0, 0.1),
     'L0_tok_ln2_g': (1.0, 0.2),
     'L0_tok_ln2_b': (0.0, 0.1),
     'L0_ffn_ln1_g': (1.0, 0.6),
     'L0_ffn_ln1_b': (0.0, 0.8),
     'L0_ffn_in_b': (0.0, 0.576),
     'L0_ffn_out_b': (0.0, 0.27),
     'L0_ffn_mlp_b1': (0.0, 0.459),
     'L0_ffn_mlp_b2': (0.0, 0.1),
     'L0_ffn_ln2_g': (1.0, 0.6),
     'L0_ffn_ln2_b': (0.0, 0.728),
     'L0_ffn_gate_b': (0.0, 0.364),
     'L0_ffn_exp_b1': (0.0, 0.738),
     'L0_ffn_exp_b2': (0.0, 0.37)}
    factors = {'L0_attn_b_qkv': 2.842,
     'L0_attn_b_proj': 3.045,
     'L0_ffn_in_w': 5.776,
     'L0_ffn_out_w': 3.279}
    for name, (base, spread) in spreads.items():
        noise = np.random.default_rng([zlib.crc32(name.encode()), seed]).standard_normal(out[name].shape)
        drawn = base * np.exp(spread * noise) if base else spread * noise
        out[name] = jnp.asarray(drawn.astype(out[name].dtype))
    for name, factor in factors.items():
        out[name] = (out[name] * factor).astype(out[name].dtype)
    return out
```

```python
import itertools
from contextlib import ExitStack

import concourse.bass as bass
from concourse import mybir

ALU = mybir.AluOpType
ACT = mybir.ActivationFunctionType
AX = mybir.AxisListType
F32 = mybir.dt.float32
F16 = mybir.dt.float16

EPS = 1e-5
WSCALE = 16.0
RSQRT_OPS = 2
COUNT_NAMES = itertools.count()


def wait(eng, sem, value):
    if not isinstance(value, int) or value > 0:
        eng.wait_ge(sem, value)


def rsqrt(pool, done, base, var, y, eps, minus_half):
    pool.tensor_tensor(y, var, eps, ALU.add).then_inc(done, 1)
    pool.wait_ge(done, base + 1)
    pool.tensor_tensor(y, y, minus_half, ALU.pow).then_inc(done, 1)


def waits(eng, *counts):
    with ExitStack() as ctx:
        known = []
        for sem, value in counts:
            if not isinstance(value, int):
                reg = ctx.enter_context(eng.register(f"count{next(COUNT_NAMES)}"))
                eng.reg_mov(reg, value)
                value = reg
            known.append((sem, value))
        for sem, value in known:
            wait(eng, sem, value)


def attention_phase(nc, name, src, dst, dst_ln, w_qkv, b_qkv, w_proj, b_proj, head_major, affine, heads=12):
    n_tok, dim = src.shape
    tok = 196
    half_t = tok // 2
    unit_t = 2 * tok
    NU = n_tok // unit_t
    hd = dim // heads
    pairs = heads // 2
    rows_q = 96
    tail = dim - 128
    SLOTS = 2 * heads
    MROW = 2048.0
    SUMS = 4 * heads
    ISCALE = 4096.0
    assert ISCALE / WSCALE < 60000 and SUMS <= 64
    STACK = 3 * hd
    sm_scale = hd ** -0.5 / (WSCALE * WSCALE)
    assert 2 * STACK == 96 and unit_t <= 512

    def scratch(label, shape, dt):
        return nc.dram_tensor(f"{name}_{label}", shape, dt, kind="Internal").ap()

    qk_scr = scratch("qk", (2, 2, 2, dim, unit_t), F16)
    m_scr = scratch("m", (2, 2, heads, tok), F16)

    with ExitStack() as ctx:
        def sb(label, shape, dt):
            return ctx.enter_context(nc.sbuf_tensor(f"{name}_{label}", shape, dt))

        def ps(label, shape, dt=F32):
            return ctx.enter_context(nc.psum_tensor(f"{name}_{label}", shape, dt))

        def sem(label):
            return ctx.enter_context(nc.semaphore(f"{name}_{label}"))

        ident = sb("ident", [128, 128], F32)
        spread = sb("spread", [128, SUMS // 4, 128], F16)
        diag = sb("diag", [128, 2], F32)
        lo_mask = sb("lo_mask", [128, 1], F32)
        wraw = sb("wraw", [rows_q, 6, 256], F32)
        praw = sb("praw", [rows_q, 2, heads, 32], F32)
        wf = sb("wf", [128, 2, 3 * dim], F32)
        wh = sb("wh", [128, 2, 3 * dim], F16)
        wl = sb("wl", [128, 2, 3 * dim], F16)
        pf = sb("pf", [128, 3, dim], F32)
        ph = sb("ph", [128, 3, dim], F16)
        pl = sb("pl", [128, 3, dim], F16)
        bq = sb("bq", [rows_q, 4], F32)
        bq16 = sb("bq16", [rows_q, 4], F32)
        bv = sb("bv", [half_t, dim], F32)
        bv16 = sb("bv16", [half_t, heads, hd], F32)
        gcol = sb("gcol", [128, 2], F32)
        bcol = sb("bcol", [128, 2], F32)
        xin = [sb(f"xin{i}", [half_t, 4, dim], F32) for i in range(2)]
        stats = sb("stats", [half_t, 4, 6], F32)
        mv = sb("mv", [half_t, 4, 2], F32)
        rstd = sb("rstd", [half_t, 4], F32)
        eps = sb("eps", [half_t, 4], F32)
        minus_half = sb("minus_half", [half_t, 4], F32)
        spacer = sb("spacer", [half_t, 1], F32)
        xn = sb("xn", [half_t, 4, 256], F32)
        xf = sb("xf", [128, 2, unit_t], F32)
        xh = [sb(f"xh{i}", [128, 2, unit_t], F16) for i in range(2)]
        xl = [sb(f"xl{i}", [128, 2, unit_t], F16) for i in range(2)]
        qkh = sb("qkh", [rows_q, 4, unit_t], F16)
        qkl = sb("qkl", [rows_q, 4, unit_t], F16)
        qst = [sb(f"qst{i}", [98, pairs, unit_t], F16) for i in range(2)]
        kst = [sb(f"kst{i}", [98, pairs, 2, unit_t], F16) for i in range(2)]
        vp = [sb(f"vp{i}", [half_t, 4, heads, 32], F32) for i in range(2)]
        mx = sb("mx", [half_t, 2, 2, heads], F32)
        negm = sb("negm", [half_t, 2, 2, heads], F32)
        mrow = sb("mrow", [heads, 2, tok], F16)
        pt = [sb(f"pt{i}", [half_t, 2, tok], F32) for i in range(4)]
        ctxs = [sb(f"ctxs{i}", [128, 3, unit_t], F32) for i in range(2)]
        sums = sb("sums", [128, half_t], F32)
        inv = sb("inv", [128, half_t], F32)
        inv_hi = sb("inv_hi", [128, half_t], F16)
        inv_st = sb("inv_st", [128, half_t], F16)
        rec = sb("rec", [128, 3, unit_t], F32)
        cn = sb("cn", [128, 3, unit_t], F32)
        ch = sb("ch", [128, 3, unit_t], F16)
        cl = sb("cl", [128, 3, unit_t], F16)
        xres = sb("xres", [half_t, 4, dim], F32)
        xo = sb("xo", [half_t, 4, dim], F32)
        ostats = sb("ostats", [half_t, 4, 6], F32)
        omv = sb("omv", [half_t, 4, 2], F32)
        orstd = sb("orstd", [half_t, 4], F32)
        xo_ln = sb("xo_ln", [half_t, 4, dim], F32)

        misc = [ps(f"misc{i}", [128, 512]) for i in range(2)]
        st_ps = [ps(f"st{i}", [128, 512]) for i in range(2)]
        mx_ps = [ps(f"mxp{i}", [128, 512]) for i in range(2)]
        pv_ps = [ps(f"pv{i}", [128, 512]) for i in range(2)]

        w_in = sem("w_in")
        consts = sem("consts")
        w_t = sem("w_t")
        w_f = sem("w_f")
        w_ok = sem("w_ok")
        x_in = sem("x_in")
        stat_s = sem("stat_s")
        mv_s = sem("mv_s")
        rsqrt_s = sem("rsqrt_s")
        xn_s = sem("xn_s")
        xt_s = sem("xt_s")
        xf_s = sem("xf_s")
        xh_s = sem("xh_s")
        xl_s = sem("xl_s")
        qk_s = sem("qk_s")
        qh_s = sem("qh_s")
        ql_s = sem("ql_s")
        scr_s = [sem(f"scr_s{i}") for i in range(2)]
        stk_s = [[sem(f"stk_s{i}{a}") for a in range(2)] for i in range(2)]
        v_s = sem("v_s")
        vp_s = sem("vp_s")
        mm_s = sem("mm_s")
        mx_s = sem("mx_s")
        nm_s = sem("nm_s")
        mt_s = sem("mt_s")
        mr_s = sem("mr_s")
        mo_s = sem("mo_s")
        ms_s = [sem(f"ms_s{a}") for a in range(2)]
        st_s = sem("st_s")
        exp_s = sem("exp_s")
        pv_s = sem("pv_s")
        ctx_s = sem("ctx_s")
        sum_s = sem("sum_s")
        inv_s = sem("inv_s")
        r_s = sem("r_s")
        rec_s = sem("rec_s")
        cn_s = sem("cn_s")
        ch_s = sem("ch_s")
        cl_s = sem("cl_s")
        pr_s = sem("pr_s")
        xres_s = sem("xres_s")
        xo_s = sem("xo_s")
        out_s = sem("out_s")
        if dst_ln is not None:
            ostat_s, omv_s, orsqrt_s, oln_s, outl_s = (sem(x) for x in ("ostat_s", "omv_s", "orsqrt_s", "oln_s", "outl_s"))
        INV, NORM = 3, 5
        LAG = {"X": 4, "L": 3, "P": 2, "M": 1, "C": 0, "O": -1, "Z": -2}

        USES = {
            "mT1": (1, "C", mr_s, 2, 2), "QK0": (0, "P", ql_s, 4, 1), "R0": (1, "O", rec_s, 3, 1),
            "QK1": (0, "P", ql_s, 4, 2), "R1": (1, "O", rec_s, 3, 2), "QK2": (0, "P", ql_s, 4, 3),
            "R2": (1, "O", rec_s, 3, 3), "QK3": (0, "P", ql_s, 4, 4), "mT0": (0, "M", mr_s, 2, 1),
            "PR0": (1, "O", xo_s, 2, 1), "PR1": (0, "O", xo_s, 2, 2), "V0": (1, "M", vp_s, 2, 1),
            "T0": (0, "L", xf_s, 2, 1), "V1": (1, "M", vp_s, 2, 2), "T1": (0, "L", xf_s, 2, 2),
        }
        BANK = {use: v[0] for use, v in USES.items()}

        QK_AT, SPREAD_AT, PROJ_AT, V_AT, TURN_AT = (3, 6, 9, 11), (7, 9, 10), (16, 17), (18, 21), (20, 22)

        STATS_AT, NORM_AT, LAST_AT = (2, 3, 5, 8), (13, 14, 15, 16), (9, 11, 14, 15)

        def last_reader(use, step):
            order = [u for u in USES if BANK[u] == BANK[use]]
            for back in range(1, 4 * len(order)):
                at = order.index(use) - back
                _, kind, s, per_unit, this = USES[order[at % len(order)]]
                unit = step + at // len(order) + LAG[kind]
                if not isinstance(unit, int) or 0 <= unit < NU:
                    return s, per_unit * unit + this
            return None

        def steps(eng, body):
            def kinds(s):
                return {k for k, lag in LAG.items() if 0 <= s + lag < NU}
            first, last = 3, NU - 4
            pairs_n = (last - first) // 2
            for s in range(-4, min(first, NU + 3)):
                body(s, s % 2, kinds(s))
            stop = first
            if pairs_n > 0:
                stop = first + 2 * pairs_n
                with eng.Fori(0, pairs_n) as i:
                    body(2 * i + first, first % 2, set(LAG))
                    body(2 * i + first + 1, (first + 1) % 2, set(LAG))
            for s in range(stop, NU + 3):
                body(s, s % 2, kinds(s))

        g_rows = src.rearrange("(t p) d -> p t d", p=half_t)
        o_rows = dst.rearrange("(t p) d -> p t d", p=half_t)
        l_rows = dst_ln.rearrange("(t p) d -> p t d", p=half_t) if dst_ln is not None else None
        block = ctx.enter_context(nc.Block())

        n_w_loads = (14 if head_major else 3) + 2 + 2 + 1 + (2 * 3 if affine is not None else 0)

        def halves(rows):
            qk = rows[0:2 * dim]
            v = qk.rearrange("(w h d) c -> w d h c", w=2, h=heads) if len(rows.shape) == 2 else qk.rearrange("(w h d) -> w d h", w=2, h=heads)
            return [v[w, m * (hd // 2):(m + 1) * (hd // 2)] for w in range(2) for m in range(2)]

        @block.sync
        def _(sp):
            w_rows = w_qkv.rearrange("(r p) c -> p r c", p=rows_q)
            if head_major:
                for r, part in enumerate(halves(w_qkv)):
                    sp.dma_start(wraw[:, r, 0:dim], part).then_inc(w_in, 16)
                    sp.dma_start(wraw[:, r, dim:256], part[:, :, 128:dim]).then_inc(w_in, 16)
                sp.dma_start(wraw[:, 4:6, 0:dim], w_rows[:, 4:6]).then_inc(w_in, 16)
                sp.dma_start(wraw[:, 4:6, dim:256], w_rows[:, 4:6, 128:dim]).then_inc(w_in, 16)
                for r, part in enumerate(halves(b_qkv)):
                    sp.dma_start(bq[:, r:r + 1], part.unsqueeze(2), allow_slow_non_contiguous=True).then_inc(w_in, 16)
            else:
                sp.dma_start(wraw[:, :, 0:dim], w_rows).then_inc(w_in, 16)
                sp.dma_start(wraw[:, :, dim:256], w_rows[:, :, 128:dim]).then_inc(w_in, 16)
                sp.dma_start(bq[:], b_qkv[0:4 * rows_q].rearrange("(m p) -> p m", p=rows_q),
                             allow_slow_non_contiguous=True).then_inc(w_in, 16)
            sp.wait_ge(consts, 1)
            for e in range(2):
                sp.dma_start(praw[:, e, :, 0:hd],
                             w_proj[e * rows_q:(e + 1) * rows_q, :].rearrange("p (h d) -> p h d", h=heads)).then_inc(w_in, 16)
                sp.dma_start(praw[:, e, 0, hd + 1:hd + 2],
                             b_proj[e * rows_q:(e + 1) * rows_q].rearrange("(p o) -> p o", o=1)).then_inc(w_in, 16)
            bv_row = b_qkv[2 * dim:3 * dim]
            sp.dma_start(bv[:], bv_row.partition_broadcast(half_t)).then_inc(w_in, 16)
            if affine is not None:
                for col, vec in ((gcol, affine[0]), (bcol, affine[1])):
                    v = vec.rearrange("(p o) -> p o", o=1)
                    sp.dma_start(col[:, 0:1], v[0:128]).then_inc(w_in, 16)
                    for part in range(2):
                        sp.dma_start(col[part * tail:(part + 1) * tail, 1:2], v[128:dim]).then_inc(w_in, 16)

            def step(s, par, kinds):
                if "O" in kinds:
                    u, b = s - 1, (par + 1) % 2
                    wait(sp, xo_s, 2 * u)
                    sp.dma_start(xres[:], g_rows[:, bass.ds(u * 4, 4), :]).then_inc(xres_s, 16)
                    waits(sp,
                          (ctx_s, 6 * (u + 1)),
                          (inv_s, INV * u))
                    for at in (0, 64):
                        sp.dma_start(sums[at:at + SUMS, :],
                                     ctxs[b][hd::32].rearrange("h g (q t) -> h (g q) t", q=4)).then_inc(sum_s, 16)
                if "C" in kinds:
                    store_maxima(s, par, 1)
                if "M" in kinds:
                    load_stacks(s + 1, (par + 1) % 2, 1, 0)
                if "C" in kinds:
                    load_maxima(s, par, 1)
                if "M" in kinds:
                    load_stacks(s + 1, (par + 1) % 2, 1, 1)
                if "P" in kinds:
                    u = s + 2
                    for which in range(2):
                        waits(sp,
                              (ql_s, 4 * u + 2 * which + 2),
                              *((stk_s[which][a], 64 * (u - 1)) for a in range(2)))
                        for hl, t in enumerate((qkh, qkl)):
                            sp.dma_start(qk_scr[par, which, hl].rearrange("(m p) t -> p m t", p=rows_q),
                                         t[:, 2 * which:2 * which + 2, :]).then_inc(scr_s[which], 16)
                    load_stacks(u, par, 0, 0)
                if "M" in kinds:
                    store_maxima(s + 1, (par + 1) % 2, 0)
                if "P" in kinds:
                    load_stacks(s + 2, par, 0, 1)
                if "M" in kinds:
                    load_maxima(s + 1, (par + 1) % 2, 0)
                if "X" in kinds:
                    u = s + 4
                    waits(sp,
                          (xn_s, NORM * (u - 1)),
                          (stat_s, 4 * u))
                    sp.dma_start(xin[par][:], g_rows[:, bass.ds(u * 4, 4), :]).then_inc(x_in, 16)
                if "O" in kinds:
                    u = s - 1
                    wait(sp, xo_s, 2 * (u + 1))
                    sp.dma_start(o_rows[:, bass.ds(u * 4, 4), :], xo[:]).then_inc(out_s, 16)
                if "Z" in kinds and l_rows is not None:
                    u = s - 2
                    wait(sp, oln_s, 4 * (u + 1))
                    sp.dma_start(l_rows[:, bass.ds(u * 4, 4), :], xo_ln[:]).then_inc(outl_s, 16)

            def load_stacks(u, b, a, which):
                cols = slice(a * tok, (a + 1) * tok)
                waits(sp,
                      (st_s, SLOTS * (u - 2) + (a + 1) * heads),
                      (scr_s[which], 32 * (u + 1)),
                      (stk_s[which][a], 64 * u))
                for j in range(2):
                    for slot, parts in ((0, 1), (1, 2)) if which == 0 else ((2, 1), (0, 2)):
                        at = slice(j * STACK + slot * hd, j * STACK + (slot + parts) * hd)
                        rows = qk_scr[b, which, 0:parts, :, cols].rearrange("h (d p j) t -> j h d p t", j=2, d=hd)[j]
                        dest = qst[b][at, :, cols] if which == 0 else kst[b][at, :, j, cols]
                        sp.dma_start(dest, rows).then_inc(stk_s[which][a], 16)

            def store_maxima(u, b, a):
                wait(sp, mr_s, 2 * u + a + 1)
                sp.dma_start(m_scr[b, a], mrow[:, a, :]).then_inc(mo_s, 16)

            def load_maxima(u, b, a):
                waits(sp,
                      (mo_s, 16 * (2 * u + a + 1)),
                      (ms_s[a], 16 * u))
                sp.dma_start(qst[b][96:98, :, a * tok:(a + 1) * tok],
                             m_scr[b, a].rearrange("(p j) t -> j p t", j=2)).then_inc(ms_s[a], 16)

            steps(sp, step)
            sp.wait_ge(out_s, 16 * NU)
            if l_rows is not None:
                sp.wait_ge(outl_s, 16 * NU)

        @block.gpsimd
        def _(pool):
            pool.memset(praw[:], 0.0).then_inc(consts, 1)
            pool.memset(ident[:], 0.0).then_inc(consts, 1)
            pool.memset(spread[:], 0.0).then_inc(consts, 1)
            pool.memset(diag[:], 0.0).then_inc(consts, 1)
            pool.memset(sums[:], 1.0).then_inc(consts, 1)
            pool.memset(lo_mask[:], -1.0).then_inc(consts, 1)
            pool.memset(eps[:], EPS).then_inc(consts, 1)
            pool.memset(minus_half[:], -0.5).then_inc(consts, 1)
            pool.wait_ge(consts, 8)
            pool.memset(lo_mask[0:64, :], 0.0).then_inc(consts, 1)
            pool.wait_ge(consts, 9)
            pool.affine_select(out=ident[:], in_=ident[:], compare_op=ALU.not_equal, fill=1.0, base=0,
                               pattern=[[-1, 128]], channel_multiplier=1).then_inc(consts, 1)
            pool.affine_select(out=diag[:], in_=diag[:], compare_op=ALU.not_equal, fill=MROW, base=-96,
                               pattern=[[-1, 2]], channel_multiplier=1).then_inc(consts, 1)
            rows = spread[:].rearrange("p n (h r) -> p n h r", h=4)
            for part in range(2):
                pool.affine_select(out=rows, in_=rows, compare_op=ALU.not_equal, fill=1.0, base=-64 * part,
                                   pattern=[[-1, SUMS // 4], [-SUMS // 4, 4], [0, 32]], channel_multiplier=1).then_inc(consts, 1)
                pool.wait_ge(consts, 12 + part)

            def step(s, par, kinds):
                if "O" not in kinds and "L" in kinds:
                    layer_norm_scale(s + 3)
                if "O" in kinds:
                    u = s - 1
                    b = (par + 1) % 2
                    for g in (0, 1, 2, None):
                        if g == 1 and "L" in kinds:
                            layer_norm_scale(s + 3)
                        if g is not None:
                            wait(pool, rec_s, 3 * u + g + 1)
                            wait(pool, cl_s, 3 * (u - 1) + g + 1)
                            pool.tensor_tensor(cn[:, g, :], ctxs[b][:, g, :], rec[:, g, :], ALU.mult).then_inc(cn_s, 1)
                        for low in {0: (), 1: (0,), 2: (1,), None: (2,)}[g]:
                            wait(pool, ch_s, 3 * u + low + 1)
                            wait(pool, pr_s, 2 * u)
                            pool.tensor_tensor(cl[:, low, :], cn[:, low, :], ch[:, low, :], ALU.subtract).then_inc(cl_s, 1)
                if "O" in kinds and l_rows is not None:
                    u = s - 1
                    wait(pool, omv_s, 4 * (u + 1))
                    wait(pool, oln_s, 4 * u)
                    rsqrt(pool, orsqrt_s, u * RSQRT_OPS, omv[:, :, 1], orstd[:], eps[:], minus_half[:])

            def layer_norm_scale(u):
                wait(pool, mv_s, 4 * (u + 1))
                wait(pool, xn_s, NORM * u)
                rsqrt(pool, rsqrt_s, u * RSQRT_OPS, mv[:, :, 1], rstd[:], eps[:], minus_half[:])

            steps(pool, step)

        @block.scalar
        def _(act):
            act.wait_ge(w_in, 16 * n_w_loads)
            act.mul(bq16[:], bq[:], WSCALE).then_inc(w_f, 1)
            act.mul(bv16[:], bv[:].rearrange("p (h d) -> p h d" if head_major else "p (d h) -> p h d", h=heads), WSCALE).then_inc(w_f, 1)
            for n in range(4):
                act.wait_ge(w_t, n + 1)
                act.mul(wf[:, n // 2, (n % 2) * 288:(n % 2) * 288 + 288], misc[n % 2][:, 0:288], WSCALE).then_inc(w_f, 1)
            for n in range(3):
                act.wait_ge(w_t, n + 5)
                act.mul(pf[:, n, :], misc[n % 2][:, 0:dim], WSCALE).then_inc(w_f, 1)

            def step(s, par, kinds):
                for k in range(SLOTS):
                    if k == 2 and "C" in kinds:
                        maxima_row(s, 1)
                    if k == 15 and "M" in kinds:
                        maxima_row(s + 1, 0)
                    if "O" in kinds and k - 1 in SPREAD_AT:
                        u, g = s - 1, SPREAD_AT.index(k - 1)
                        wait(act, r_s, 3 * u + g + 1)
                        wait(act, cn_s, 3 * (u - 1) + g + 1)
                        act.mul(rec[:, g, :], misc[1][:, 0:unit_t], 1.0 / ISCALE).then_inc(rec_s, 1)
                    if "P" in kinds and k - 1 in QK_AT:
                        u, m = s + 2, QK_AT.index(k - 1)
                        wait(act, qk_s, 4 * u + m + 1)
                        wait(act, scr_s[m // 2], 32 * u)
                        act.activation(qkh[:, m, :], misc[0][0:rows_q, 0:unit_t], ACT.Identity,
                                       bias=bq16[:, m:m + 1]).then_inc(qh_s, 1)
                    if "L" in kinds and k - 1 in TURN_AT:
                        u, part = s + 3, TURN_AT.index(k - 1)
                        wait(act, xt_s, 2 * u + part + 1)
                        wait(act, xl_s, 2 * (u - 1) + part + 1)
                        if affine is None:
                            act.copy(xf[:, part, :], misc[0][:, 0:unit_t]).then_inc(xf_s, 1)
                        else:
                            act.activation(xf[:, part, :], misc[0][:, 0:unit_t], ACT.Identity,
                                           scale=gcol[:, part:part + 1], bias=bcol[:, part:part + 1]).then_inc(xf_s, 1)
                    if "C" in kinds:
                        n = SLOTS * s + k
                        wait(act, st_s, n + 1)
                        wait(act, pv_s, n - 3)
                        act.activation(pt[k % 4][:].rearrange("p a t -> p (a t)"), st_ps[k % 2][0:half_t, 0:unit_t],
                                       ACT.Exp, scale=sm_scale).then_inc(exp_s, 1)
                    if k % 4 == 2:
                        u, b, g6, on = (s - 1, (par + 1) % 2, 5, "O") if k == 2 else (s, par, k // 4 - 1, "C")
                        if on in kinds:
                            a, g = g6 // 3, g6 % 3
                            wait(act, pv_s, SLOTS * u + 4 * (g6 + 1))
                            wait(act, cn_s, 3 * (u - 1))
                            act.copy(ctxs[b][:, g, a * tok:(a + 1) * tok], pv_ps[g6 % 2][:, 0:tok]).then_inc(ctx_s, 1)
                    if "L" in kinds and k == 23 or "P" in kinds and k == 0:
                        u, b, part = (s + 3, (par + 1) % 2, 0) if k else (s + 2, par, 1)
                        wait(act, xf_s, 2 * u + part + 1)
                        wait(act, v_s, 2 * (u - 1))
                        act.copy(xh[b][:, part, :], xf[:, part, :]).then_inc(xh_s, 1)
                    if "O" in kinds and k - 3 in SPREAD_AT:
                        u, g = s - 1, SPREAD_AT.index(k - 3)
                        wait(act, cn_s, 3 * u + g + 1)
                        wait(act, pr_s, 2 * u)
                        act.copy(ch[:, g, :], cn[:, g, :]).then_inc(ch_s, 1)

            def maxima_row(u, a):
                wait(act, mt_s, 2 * u + a + 1)
                wait(act, mo_s, 16 * (2 * u + a - 1))
                act.copy(mrow[:, a, :], misc[1 if a else 0][0:heads, 0:tok]).then_inc(mr_s, 1)

            steps(act, step)

        @block.vector
        def _(dve):
            for i in range(2):
                dve.memset(kst[i][:], 0.0).then_inc(w_ok, 1)
                dve.memset(vp[i][:], WSCALE).then_inc(w_ok, 1)
            dve.wait_ge(w_ok, 4)
            dve.wait_ge(consts, 13)
            for i in range(2):
                dve.memset(vp[i][:, :, :, hd:hd + 1], WSCALE / ISCALE).then_inc(w_ok, 1)
                for j in range(2):
                    v = kst[i][96:98, :, j, :]
                    dve.tensor_scalar(v, v, diag[96:98, j:j + 1], None, ALU.add).then_inc(w_ok, 1)
            dve.wait_ge(w_f, 6)
            dve.tensor_copy(wh[:], wf[:]).then_inc(w_ok, 1)
            dve.wait_ge(w_f, 9)
            dve.tensor_copy(ph[:], pf[:]).then_inc(w_ok, 1)
            dve.wait_ge(w_ok, 11)
            dve.tensor_tensor(wl[:], wf[:], wh[:], ALU.subtract).then_inc(w_ok, 1)
            dve.wait_ge(w_ok, 12)
            dve.tensor_tensor(pl[:], pf[:], ph[:], ALU.subtract).then_inc(w_ok, 1)

            def step(s, par, kinds):
                for k in range(SLOTS):
                    if k == 0 and "C" in kinds:
                        negated_maxima(s, 1)
                    if "M" in kinds:
                        u = s + 1
                        a, qt, p = k // heads, (k // pairs) % 2, k % pairs
                        wait(dve, mm_s, SLOTS * u + k + 1)
                        if k % heads == 0:
                            wait(dve, nm_s, 2 * u - 1 + a)
                        dve.tensor_reduce(mx[:, a, qt, 2 * p:2 * p + 2],
                                          mx_ps[k % 2][0:half_t, 0:unit_t].rearrange("p (j t) -> p j t", j=2),
                                          AX.X, ALU.max).then_inc(mx_s, 1)
                    if k == 12 and "M" in kinds:
                        negated_maxima(s + 1, 0)
                    if "P" in kinds:
                        u, b = s + 2, par
                        if k in (0, 1):
                            part = k
                            wait(dve, xh_s, 2 * u + part + 1)
                            wait(dve, v_s, 2 * (u - 1))
                            if part == 0:
                                dve.tensor_tensor(xl[b][:, 0, :], xf[:, 0, :], xh[b][:, 0, :], ALU.subtract).then_inc(xl_s, 1)
                            else:
                                dve.scalar_tensor_tensor(out=xl[b][:, 1, :], in0=xh[b][:, 1, :], scalar=lo_mask[:, 0:1],
                                                         in1=xf[:, 1, :], op0=ALU.mult, op1=ALU.add).then_inc(xl_s, 1)
                        if k - 1 in QK_AT:
                            m = QK_AT.index(k - 1)
                            wait(dve, qh_s, 4 * u + m + 1)
                            wait(dve, scr_s[m // 2], 32 * u)
                            dve.scalar_tensor_tensor(out=qkl[:, m, :], in0=misc[0][0:rows_q, 0:unit_t],
                                                     scalar=bq16[:, m:m + 1], in1=qkh[:, m, :],
                                                     op0=ALU.add, op1=ALU.subtract).then_inc(ql_s, 1)
                    if "L" in kinds:
                        u, b = s + 3, (par + 1) % 2
                        if k in STATS_AT:
                            t = STATS_AT.index(k)
                            if t == 0:
                                wait(dve, x_in, 16 * (u + 1))
                                wait(dve, mv_s, 4 * u)
                            dve.bn_stats(stats[:, t, :], xin[b][:, t, :]).then_inc(stat_s, 1)
                        if k == 9:
                            wait(dve, rsqrt_s, RSQRT_OPS * u)
                            wait(dve, xn_s, NORM * u)
                            wait(dve, stat_s, 4 * (u + 1))
                            dve.memset(spacer[:], 0.0)
                            for t in range(4):
                                dve.bn_aggr(mv[:, t, :], stats[:, t, :]).then_inc(mv_s, 1)
                        if k in NORM_AT:
                            t = NORM_AT.index(k)
                            if t == 0:
                                wait(dve, rsqrt_s, RSQRT_OPS * (u + 1))
                                wait(dve, xt_s, 2 * u)
                            dve.tensor_scalar(xn[:, t, 0:dim], xin[b][:, t, :], mv[:, t, 0:1], rstd[:, t:t + 1],
                                              ALU.subtract, ALU.mult).then_inc(xn_s, 1)
                        if k == NORM_AT[3] + 1:
                            wait(dve, xn_s, NORM * u + 4)
                            dve.tensor_copy(xn[:, :, dim:256], xn[:, :, 128:dim]).then_inc(xn_s, 1)
                    if "M" in kinds and k - 1 in V_AT:
                        u, b, n = s + 1, (par + 1) % 2, V_AT.index(k - 1)
                        wait(dve, v_s, 2 * u + n + 1)
                        wait(dve, pv_s, SLOTS * (u - 1))
                        order = "p (x h d) -> p x h d" if head_major else "p (x d h) -> p x h d"
                        v = misc[1][0:half_t, 0:2 * dim].rearrange(order, x=2, h=heads)
                        for x in range(2):
                            ins = dve.tensor_tensor(vp[b][:, 2 * n + x, :, 0:hd], v[:, x], bv16[:], ALU.add)
                        ins.then_inc(vp_s, 1)
                    if "O" in kinds:
                        u = s - 1
                        if k == SPREAD_AT[0] - 1:
                            wait(dve, sum_s, 32 * (u + 1))
                            wait(dve, r_s, 3 * u)
                            dve.reciprocal(inv[:], sums[:]).then_inc(inv_s, 1)
                            wait(dve, inv_s, INV * u + 1)
                            dve.tensor_copy(inv_hi[:], inv[:]).then_inc(inv_s, 1)
                            wait(dve, inv_s, INV * u + 2)
                            dve.scalar_tensor_tensor(out=inv_st[:], in0=inv_hi[:], scalar=lo_mask[:, 0:1], in1=inv[:],
                                                     op0=ALU.mult, op1=ALU.add).then_inc(inv_s, 1)
                        if k - 1 in PROJ_AT:
                            n = PROJ_AT.index(k - 1)
                            wait(dve, pr_s, 2 * u + n + 1)
                            wait(dve, xres_s, 16 * (u + 1))
                            wait(dve, out_s, 16 * u)
                            if l_rows is not None:
                                wait(dve, oln_s, 4 * u)
                            dve.scalar_tensor_tensor(out=xo[:, 2 * n:2 * n + 2, :],
                                                     in0=misc[BANK[f"PR{n}"]][0:half_t, 0:2 * dim].rearrange("p (x d) -> p x d", x=2),
                                                     scalar=1.0 / WSCALE, in1=xres[:, 2 * n:2 * n + 2, :],
                                                     op0=ALU.mult, op1=ALU.add).then_inc(xo_s, 1)
                        if l_rows is not None:
                            if k - 2 in PROJ_AT:
                                n = PROJ_AT.index(k - 2)
                                wait(dve, xo_s, 2 * u + n + 1)
                                for t in (2 * n, 2 * n + 1):
                                    dve.bn_stats(ostats[:, t, :], xo[:, t, :]).then_inc(ostat_s, 1)
                            if k == 20:
                                wait(dve, ostat_s, 4 * (u + 1))
                                dve.memset(spacer[:], 0.0)
                                for t in range(4):
                                    dve.bn_aggr(omv[:, t, :], ostats[:, t, :]).then_inc(omv_s, 1)
                    if "Z" in kinds and l_rows is not None and k in LAST_AT:
                        u, t = s - 2, LAST_AT.index(k)
                        if t == 0:
                            wait(dve, orsqrt_s, RSQRT_OPS * (u + 1))
                            wait(dve, outl_s, 16 * u)
                        dve.tensor_scalar(xo_ln[:, t, :], xo[:, t, :], omv[:, t, 0:1], orstd[:, t:t + 1],
                                          ALU.subtract, ALU.mult).then_inc(oln_s, 1)

            def negated_maxima(u, a):
                wait(dve, mx_s, SLOTS * u + heads * (a + 1))
                wait(dve, mt_s, 2 * u + a - 1)
                dve.tensor_scalar(negm[:, a], mx[:, a], -1.0 / MROW, None, ALU.mult).then_inc(nm_s, 1)

            steps(dve, step)

        @block.tensor
        def _(pe):
            pe.wait_ge(consts, 13)
            pe.wait_ge(w_in, 16 * n_w_loads)
            for n in range(4):
                part, half = n // 2, n % 2
                if n >= 2:
                    pe.wait_ge(w_f, 2 + n - 1)
                for r in range(3):
                    w = wraw[:, 3 * half + r, part * 128:(part + 1) * 128]
                    ins = pe.transpose(misc[n % 2][:, r * rows_q:(r + 1) * rows_q], w, ident[0:rows_q, 0:rows_q])
                ins.then_inc(w_t, 1)
            for g in range(3):
                pe.wait_ge(w_f, 2 + 4 + g - 1)
                for e in range(2):
                    w = praw[:, e, 4 * g:4 * g + 4, :].rearrange("p h r -> p (h r)")
                    ins = pe.transpose(misc[g % 2][:, e * rows_q:(e + 1) * rows_q], w, ident[0:rows_q, 0:rows_q])
                ins.then_inc(w_t, 1)
            pe.wait_ge(w_ok, 14)
            pe.wait_ge(w_f, 9)

            def step(s, par, kinds):
                def take(use):
                    last = last_reader(use, s)
                    if last is not None:
                        wait(pe, *last)
                    return misc[BANK[use]]

                for k in range(SLOTS):
                    a, h = k // heads, k % heads
                    cols = slice(a * tok, (a + 1) * tok)
                    if "C" in kinds:
                        n = SLOTS * s + k
                        if k % heads == 0:
                            wait(pe, ms_s[a], 16 * (s + 1))
                        wait(pe, exp_s, n - 1)
                        for kt in range(2):
                            ins = pe.matmul(st_ps[k % 2][0:half_t, kt * tok:(kt + 1) * tok],
                                            kst[par][:, h // 2, h % 2, a * tok + kt * half_t:a * tok + (kt + 1) * half_t],
                                            qst[par][:, h // 2, cols], start=True, stop=True)
                        ins.then_inc(st_s, 1)
                    if "M" in kinds:
                        u, b = s + 1, (par + 1) % 2
                        qt, p = (k // pairs) % 2, k % pairs
                        if k % heads == 0:
                            wait(pe, stk_s[0][a], 64 * (u + 1))
                            wait(pe, stk_s[1][a], 64 * (u + 1))
                        wait(pe, mx_s, SLOTS * u + k - 1)
                        pe.matmul(mx_ps[k % 2][0:half_t, 0:unit_t],
                                  qst[b][0:96, p, a * tok + qt * half_t:a * tok + (qt + 1) * half_t],
                                  kst[b][0:96, p, :, cols], start=True, stop=True).then_inc(mm_s, 1)
                    if "P" in kinds:
                        u, b = s + 2, par
                        if k in QK_AT:
                            m = QK_AT.index(k)
                            bank = take(f"QK{m}")
                            wait(pe, xl_s, 2 * (u + 1))
                            cs = slice(m * rows_q, (m + 1) * rows_q)
                            products(pe, bank[0:rows_q, 0:unit_t],
                                     [(wh[:, 0, cs], xh[b][:, 0, :]), (wl[:, 0, cs], xh[b][:, 0, :]), (wh[:, 0, cs], xl[b][:, 0, :]),
                                      (wh[:, 1, cs], xl[b][:, 1, :]), (wl[:, 1, cs], xl[b][:, 1, :])]).then_inc(qk_s, 1)
                    if "L" in kinds and k in TURN_AT:
                        u, part = s + 3, TURN_AT.index(k)
                        bank = take(f"T{part}")
                        wait(pe, xn_s, NORM * (u + 1))
                        for t in range(4):
                            x = xn[:, t, part * 128:(part + 1) * 128]
                            ins = pe.transpose(bank[:, t * half_t:(t + 1) * half_t], x, ident[0:half_t, 0:half_t])
                        ins.then_inc(xt_s, 1)
                    if "C" in kinds and k == 1:
                        turn_maxima(take("mT1"), s, 1)
                    if "M" in kinds and k == 14:
                        turn_maxima(take("mT0"), s + 1, 0)
                    if "M" in kinds and k in V_AT:
                        u, b, n = s + 1, (par + 1) % 2, V_AT.index(k)
                        bank = take(f"V{n}")
                        wait(pe, xl_s, 2 * (u + 1))
                        for x in range(2):
                            ts = slice((2 * n + x) * half_t, (2 * n + x + 1) * half_t)
                            vs = slice(2 * dim, 3 * dim)
                            ins = products(pe, bank[0:half_t, x * dim:(x + 1) * dim],
                                           [(xh[b][:, 0, ts], wh[:, 0, vs]), (xh[b][:, 0, ts], wl[:, 0, vs]), (xl[b][:, 0, ts], wh[:, 0, vs]),
                                            (xl[b][:, 1, ts], wh[:, 1, vs]), (xl[b][:, 1, ts], wl[:, 1, vs])])
                        ins.then_inc(v_s, 1)
                    if "O" in kinds:
                        u, b = s - 1, (par + 1) % 2
                        if k in SPREAD_AT:
                            g = SPREAD_AT.index(k)
                            bank = take(f"R{g}")
                            wait(pe, inv_s, INV * (u + 1))
                            for q in range(4):
                                ins = pe.matmul(bank[:, q * half_t:(q + 1) * half_t], spread[:, 4 * g + q, :], inv_st[:], start=True, stop=True)
                            ins.then_inc(r_s, 1)
                        if k in PROJ_AT:
                            n = PROJ_AT.index(k)
                            bank = take(f"PR{n}")
                            wait(pe, cl_s, 3 * (u + 1))
                            for x in range(2):
                                ts = slice((2 * n + x) * half_t, (2 * n + x + 1) * half_t)
                                ins = products(pe, bank[0:half_t, x * dim:(x + 1) * dim],
                                               [(p[:, g, ts], w[:, g, :]) for g in range(3) for p, w in ((ch, ph), (ch, pl), (cl, ph))])
                            ins.then_inc(pr_s, 1)
                    u, b, kk, on = (s - 1, (par + 1) % 2, k - 2 + SLOTS, "O") if k < 2 else (s, par, k - 2, "C")
                    if on in kinds:
                        a, h = kk // heads, kk % heads
                        n, g6 = SLOTS * u + kk, kk // 4
                        if kk == 0:
                            wait(pe, vp_s, 2 * (u + 1))
                        if kk % 4 == 0:
                            wait(pe, ctx_s, 6 * u + g6 - 1)
                        if "C" not in kinds:
                            wait(pe, exp_s, n + 1)
                        rows = slice(32 * (h % 4), 32 * (h % 4) + 32)
                        for kt in range(2):
                            ins = pe.matmul(pv_ps[g6 % 2][rows, 0:tok], vp[b][:, 2 * a + kt, h, :], pt[kk % 4][:, kt, :],
                                            start=(kt == 0), stop=(kt == 1), tile_position=(0, 32 * (h % 4)))
                        ins.then_inc(pv_s, 1)

            def turn_maxima(bank, u, a):
                wait(pe, nm_s, 2 * u + a + 1)
                for qt in range(2):
                    ins = pe.transpose(bank[0:heads, qt * half_t:(qt + 1) * half_t], negm[:, a, qt, :], ident[0:half_t, 0:half_t])
                ins.then_inc(mt_s, 1)

            steps(pe, step)


def products(pe, out, terms):
    for i, (lhs, rhs) in enumerate(terms):
        ins = pe.matmul(out, lhs, rhs, start=(i == 0), stop=(i == len(terms) - 1))
    return ins


def tokenize_phase(nc, img, dst, ln1_g, ln1_b, w, bias, ln2_g, ln2_b):
    n_img, chans, side, _ = img.shape
    patch = 16
    cols = side // patch
    G_IMG = 8
    R = G_IMG * cols
    n_groups = n_img // G_IMG
    feats, dim = w.shape
    KT = feats // 128
    line = patch * side
    UPG = cols // 2
    NU = n_groups * UPG
    half = feats // 2
    assert n_img % G_IMG == 0 and KT % 2 == 0

    with ExitStack() as ctx:
        def sb(label, shape, dt):
            return ctx.enter_context(nc.sbuf_tensor(f"t_{label}", shape, dt))

        def ps(label, shape, dt=F32):
            return ctx.enter_context(nc.psum_tensor(f"t_{label}", shape, dt))

        def sem(label):
            return ctx.enter_context(nc.semaphore(f"t_{label}"))

        ident = sb("ident", [128, 128], F32)
        ones = sb("ones", [128, R], F32)
        wraw = sb("wraw", [128, KT, dim], F32)
        wf = sb("wf", [128, KT, dim], F32)
        wh = sb("wh", [128, KT, dim], F16)
        wl = sb("wl", [128, KT, dim], F16)
        gcol = sb("gcol", [128, KT], F32)
        bcol = sb("bcol", [128, KT], F32)
        g16 = sb("g16", [128, KT], F32)
        bspread = sb("bspread", [128, KT, R], F32)
        brow = sb("brow", [R, dim], F32)
        brow_hi = sb("brow_hi", [R, dim], F16)
        brow_parts = sb("brow_parts", [R, dim], F16)
        first_two = sb("first_two", [R, R], F16)
        row_mask = sb("row_mask", [R, 1], F32)
        bias_row = sb("bias_row", [R, dim], F32)
        g2 = sb("g2", [R, dim], F32)
        b2 = sb("b2", [R, dim], F32)
        rows = [sb(f"rows{i}", [R, chans, line], F32) for i in range(2)]
        stats = sb("stats", [R, 2, 2, 6], F32)
        mv = [sb(f"mv{i}", [R, 2, 2], F32) for i in range(2)]
        rstd = [sb(f"rstd{i}", [R, 2], F32) for i in range(2)]
        shift = [sb(f"shift{i}", [R, 2], F32) for i in range(2)]
        eps = sb("eps", [R, 2], F32)
        minus_half = sb("minus_half", [R, 2], F32)
        xn = [sb(f"xn{i}", [R, feats], F32) for i in range(2)]
        xh = [[sb(f"xh{i}{t}", [128, KT, R], F16) for t in range(2)] for i in range(2)]
        xl = [[sb(f"xl{i}{t}", [128, KT, R], F16) for t in range(2)] for i in range(2)]
        stats2 = sb("stats2", [R, 2, 6], F32)
        mv2 = [sb(f"mv2_{i}", [R, 2, 2], F32) for i in range(2)]
        spacer = sb("spacer", [R, 1], F32)
        minus_one = sb("minus_one", [R, 2], F32)
        rstd2 = [sb(f"rstd2_{i}", [R, 2], F32) for i in range(2)]
        shift2 = [sb(f"shift2_{i}", [R, 2], F32) for i in range(2)]
        eps2 = sb("eps2", [R, 2], F32)
        yn = [sb(f"yn{i}", [R, 2, dim], F32) for i in range(2)]

        turned = [ps(f"turned{i}", [128, 2, 512]) for i in range(2)]
        yp = [ps(f"yp{i}", [128, 512]) for i in range(2)]

        consts, w_in, w_ok, bp_s = sem("consts"), sem("w_in"), sem("w_ok"), sem("bp_s")
        rows_in = sem("rows_in")
        st_s, mv_s, rsqrt_s, sh_s = sem("st_s"), sem("mv_s"), sem("rsqrt_s"), sem("sh_s")
        xn_s, tr_s, xh_s, xl_s = sem("xn_s"), sem("tr_s"), sem("xh_s"), sem("xl_s")
        yp_s, sh2_s, st2_s, mv2_s, rsqrt2_s, yn_s = (sem("yp_s"), sem("sh2_s"), sem("st2_s"), sem("mv2_s"), sem("rsqrt2_s"), sem("yn_s"))
        aff, out_s = sem("aff"), sem("out_s")

        LAG = {"A": 2, "B": 1, "C": 0, "D": -1}
        BODY = 2 * UPG

        def steps(eng, body):
            def kinds(s):
                return {k for k, lag in LAG.items() if 0 <= s + lag < NU}
            first = 3
            n = (NU - 2 - first) // BODY
            for s in range(-2, first):
                body(s, s, 0, kinds(s))
            if n > 0:
                with eng.Fori(0, n) as i:
                    for c in range(first, first + BODY):
                        body(BODY * i + c, c, i, set(LAG))
            for s in range(first + BODY * max(n, 0), NU + 1):
                body(s, s, 0, kinds(s))

        def group(c, i, lag):
            g, v = divmod(c + lag, UPG)
            return 2 * i + g, g % 2, v

        def patches(buf, col):
            return buf[:].rearrange("r c (l x) -> r (c l) x", l=patch)[:, :, col * patch:(col + 1) * patch]

        out_rows = dst.rearrange("(r x) d -> r x d", x=cols)
        block = ctx.enter_context(nc.Block())

        @block.sync
        def _(sp):
            w_view = w.rearrange("(q c) e -> c q e", c=chans)
            per = feats // chans // 128
            for k in range(KT):
                c, q = divmod(k, per)
                sp.dma_start(wraw[:, k, :], w_view[c, q * 128:(q + 1) * 128, :]).then_inc(w_in, 16)
                for col, vec in ((gcol, ln1_g), (bcol, ln1_b)):
                    v = vec.rearrange("(q c) -> c q", c=chans)[c, q * 128:(q + 1) * 128].rearrange("(p o) -> p o", o=1)
                    sp.dma_start(col[:, k:k + 1], v, allow_slow_non_contiguous=True).then_inc(w_in, 16)
            for t, vec in ((bias_row, bias), (g2, ln2_g), (b2, ln2_b)):
                sp.dma_start(t[:], vec.partition_broadcast(R)).then_inc(w_in, 16)

            def load(g, b, images):
                for j in images:
                    src = img[bass.ds(g * G_IMG + j, 1)].rearrange("o c (h l) x -> (o h) c (l x)", l=patch)
                    sp.dma_start(rows[b][j * cols:(j + 1) * cols], src).then_inc(rows_in, 16)

            def step(s, c, i, kinds):
                if "B" in kinds:
                    g, gb, v = group(c, i, 1)
                    if v < G_IMG // 2 and not (isinstance(g, int) and g + 1 >= n_groups):
                        if v == 0:
                            waits(sp,
                                  (xn_s, 2 * (s + 1)),
                                  (st_s, 4 * (s + 1) + 1))
                        else:
                            wait(sp, xn_s, 2 * (s + 1))
                        load(g + 1, 1 - gb, (2 * v, 2 * v + 1))
                if "D" in kinds:
                    g, gb, v = group(c, i, -1)
                    waits(sp,
                          (aff, 2 * (s - 1) + 2),
                          (out_s, 16 * (s - 1)))
                    sp.dma_start(out_rows[bass.ds(g * R, R), 2 * v:2 * v + 2, :], yn[(c - 1) % 2][:]).then_inc(out_s, 16)

            load(0, 0, range(G_IMG))
            steps(sp, step)
            sp.wait_ge(out_s, 16 * NU)

        @block.gpsimd
        def _(pool):
            pool.memset(ident[:], 0.0).then_inc(consts, 1)
            pool.memset(ones[:], 1.0).then_inc(consts, 1)
            pool.memset(eps[:], EPS).then_inc(consts, 1)
            pool.memset(minus_half[:], -0.5).then_inc(consts, 1)
            pool.memset(minus_one[:], -1.0).then_inc(consts, 1)
            pool.memset(eps2[:], EPS * WSCALE * WSCALE).then_inc(consts, 1)
            pool.memset(first_two[:], 0.0).then_inc(consts, 1)
            pool.memset(row_mask[:], 0.0).then_inc(consts, 1)
            pool.wait_ge(consts, 8)
            pool.memset(first_two[0:2, :], 1.0).then_inc(consts, 1)
            pool.wait_ge(consts, 9)
            pool.affine_select(out=row_mask[:], in_=row_mask[:], compare_op=ALU.not_equal, fill=-1.0, base=-1,
                               pattern=[[0, 1]], channel_multiplier=1).then_inc(consts, 1)
            pool.affine_select(out=ident[:], in_=ident[:], compare_op=ALU.not_equal, fill=1.0, base=0,
                               pattern=[[-1, 128]], channel_multiplier=1).then_inc(consts, 1)

            def step(s, c, i, kinds):
                if "A" in kinds:
                    u, b = s + 2, c % 2
                    wait(pool, mv_s, 2 * (u + 1))
                    wait(pool, xn_s, 2 * (u - 1))
                    rsqrt(pool, rsqrt_s, u * RSQRT_OPS, mv[b][:, :, 1], rstd[b][:], eps[:], minus_half[:])
                    wait(pool, rsqrt_s, RSQRT_OPS * (u + 1))
                    pool.tensor_tensor(shift[b][:], mv[b][:, :, 0], rstd[b][:], ALU.mult).then_inc(sh_s, 1)
                    wait(pool, sh_s, 2 * u + 1)
                    pool.tensor_tensor(shift[b][:], shift[b][:], minus_one[:], ALU.mult).then_inc(sh_s, 1)
                if "D" in kinds:
                    u, b = s - 1, (c - 1) % 2
                    wait(pool, yn_s, 2 * (u + 1))
                    pool.tensor_tensor(yn[b][:], yn[b][:], g2[:].unsqueeze(1).to_broadcast([R, 2, dim]), ALU.mult).then_inc(aff, 1)
                    wait(pool, aff, 2 * u + 1)
                    pool.tensor_tensor(yn[b][:], yn[b][:], b2[:].unsqueeze(1).to_broadcast([R, 2, dim]), ALU.add).then_inc(aff, 1)
                if "C" in kinds:
                    u, b = s, c % 2
                    wait(pool, mv2_s, 2 * (u + 1))
                    wait(pool, yn_s, 2 * (u - 1))
                    rsqrt(pool, rsqrt2_s, u * RSQRT_OPS, mv2[b][:, :, 1], rstd2[b][:], eps2[:], minus_half[:])
                    wait(pool, rsqrt2_s, RSQRT_OPS * (u + 1))
                    pool.tensor_tensor(shift2[b][:], mv2[b][:, :, 0], rstd2[b][:], ALU.mult).then_inc(sh2_s, 1)
                    wait(pool, sh2_s, 2 * u + 1)
                    pool.tensor_tensor(shift2[b][:], shift2[b][:], minus_one[:], ALU.mult).then_inc(sh2_s, 1)

            steps(pool, step)

        @block.scalar
        def _(act):
            act.wait_ge(w_in, 16 * (3 * KT + 3))
            act.mul(g16[:], gcol[:], WSCALE).then_inc(w_ok, 1)
            act.wait_ge(w_ok, 1)
            act.wait_ge(consts, 2)
            for k in range(KT):
                act.mul(wf[:, k, :], wraw[:, k, :], g16[:, k:k + 1]).then_inc(w_ok, 1)
                act.mul(bspread[:, k, :], ones[:], bcol[:, k:k + 1]).then_inc(w_ok, 1)

            def step(s, c, i, kinds):
                if "B" in kinds:
                    u, b = s + 1, (c + 1) % 2
                    _, gb, v = group(c, i, 1)
                    for t in range(2):
                        wait(act, sh_s, 2 * (u + 1))
                        wait(act, tr_s, 2 * (u - 1) + t + 1)
                        act.activation(xn[t][:].rearrange("r (a x) -> r a x", x=patch), patches(rows[gb], 2 * v + t), ACT.Identity,
                                       scale=rstd[b][:, t:t + 1], bias=shift[b][:, t:t + 1]).then_inc(xn_s, 1)
                    for t in range(2):
                        wait(act, tr_s, 2 * u + t + 1)
                        wait(act, yp_s, u - 1)
                        act.copy(xh[b][t][:].rearrange("p (a k) r -> p a (k r)", a=2), turned[t][:, :, 0:KT // 2 * R]).then_inc(xh_s, 1)

                if "D" in kinds:
                    normalise(s - 1, (c - 1) % 2)

            def normalise(u, b):
                wait(act, sh2_s, 2 * (u + 1))
                wait(act, out_s, 16 * (u - 1))
                for t in range(2):
                    act.activation(yn[b][:, t, :], yp[b][0:R, t * dim:(t + 1) * dim], ACT.Identity,
                                   scale=rstd2[b][:, t:t + 1], bias=shift2[b][:, t:t + 1]).then_inc(yn_s, 1)

            steps(act, step)

        @block.vector
        def _(dve):
            dve.wait_ge(w_ok, 1 + 2 * KT)
            dve.tensor_copy(wh[:], wf[:]).then_inc(w_ok, 1)
            dve.wait_ge(w_ok, 2 + 2 * KT)
            dve.tensor_tensor(wl[:], wf[:], wh[:], ALU.subtract).then_inc(w_ok, 1)
            dve.wait_ge(bp_s, 1)
            dve.tensor_tensor(brow[:], yp[0][0:R, 0:dim], bias_row[:], ALU.add).then_inc(bp_s, 1)
            dve.wait_ge(bp_s, 2)
            dve.tensor_scalar(brow[:], brow[:], WSCALE, None, ALU.mult).then_inc(bp_s, 1)
            dve.wait_ge(bp_s, 3)
            dve.tensor_copy(brow_hi[:], brow[:]).then_inc(bp_s, 1)
            dve.wait_ge(bp_s, 4)
            dve.wait_ge(consts, 11)
            dve.scalar_tensor_tensor(out=brow_parts[:], in0=brow_hi[:], scalar=row_mask[:, 0:1], in1=brow[:],
                                     op0=ALU.mult, op1=ALU.add).then_inc(bp_s, 1)

            def step(s, c, i, kinds):
                if "A" in kinds:
                    u, b = s + 2, c % 2
                    g, gb, v = group(c, i, 2)
                    wait(dve, rows_in, 16 * G_IMG * (g + 1))
                    wait(dve, mv_s, 2 * u)
                    for t in range(2):
                        for h in range(2):
                            x = patches(rows[gb], 2 * v + t)[:, h * (half // patch):(h + 1) * (half // patch), :]
                            dve.bn_stats(stats[:, t, h, :], x).then_inc(st_s, 1)
                if "A" in kinds:
                    u, b = s + 2, c % 2
                    wait(dve, sh_s, 2 * (u - 1))
                    wait(dve, st_s, 4 * (u + 1))
                    dve.memset(spacer[:], 0.0)
                    for t in range(2):
                        dve.bn_aggr(mv[b][:, t, :], stats[:, t]).then_inc(mv_s, 1)
                if "B" in kinds:
                    u, b = s + 1, (c + 1) % 2
                    for t in range(2):
                        wait(dve, xh_s, 2 * u + t + 1)
                        wait(dve, yp_s, u - 1)
                        dve.tensor_tensor(xl[b][t][:].rearrange("p (a k) r -> p a (k r)", a=2), turned[t][:, :, 0:KT // 2 * R],
                                          xh[b][t][:].rearrange("p (a k) r -> p a (k r)", a=2), ALU.subtract).then_inc(xl_s, 1)
                if "C" in kinds:
                    u, b = s, c % 2
                    wait(dve, yp_s, u + 1)
                    wait(dve, mv2_s, 2 * u)
                    for t in range(2):
                        dve.bn_stats(stats2[:, t, :], yp[b][0:R, t * dim:(t + 1) * dim]).then_inc(st2_s, 1)
                    wait(dve, st2_s, 2 * (u + 1))
                    dve.memset(spacer[:], 0.0)
                    for t in range(2):
                        dve.bn_aggr(mv2[b][:, t, :], stats2[:, t, :]).then_inc(mv2_s, 1)

            steps(dve, step)

        @block.tensor
        def _(pe):
            pe.wait_ge(w_ok, 1 + 2 * KT)
            for k in range(KT):
                ins = pe.matmul(yp[0][0:R, 0:dim], bspread[:, k, :], wraw[:, k, :], start=(k == 0), stop=(k == KT - 1))
            ins.then_inc(bp_s, 1)
            pe.wait_ge(bp_s, 5)
            pe.wait_ge(consts, 11)
            pe.wait_ge(w_ok, 3 + 2 * KT)

            def step(s, c, i, kinds):
                if "B" in kinds:
                    u = s + 1
                    for t in range(2):
                        wait(pe, xn_s, 2 * u + t + 1)
                        wait(pe, xl_s, 2 * (u - 1) + t + 1)
                        for k in range(KT):
                            a, kk = divmod(k, KT // 2)
                            ins = pe.transpose(turned[t][:, a, kk * R:(kk + 1) * R], xn[t][:, k * 128:(k + 1) * 128], ident[0:R, 0:R])
                        ins.then_inc(tr_s, 1)
                if "C" in kinds:
                    u, b = s, c % 2
                    for t in range(2):
                        wait(pe, xl_s, 2 * u + t + 1)
                        if t == 0:
                            wait(pe, yn_s, 2 * (u - 1))
                        ins = products(pe, yp[b][0:R, t * dim:(t + 1) * dim],
                                       [(x[b][t][:, k, :], m[:, k, :]) for k in range(KT) for x, m in ((xh, wh), (xh, wl), (xl, wh))]
                                       + [(first_two[:], brow_parts[:])])
                    ins.then_inc(yp_s, 1)

            steps(pe, step)


def ffn_phase(nc, x3, h1, out, mlp, experts, ln_g, ln_b, gate_w, gate_b):
    n_tok, dim = x3.shape
    hid = mlp[0].shape[1]
    n_exp = experts[0].shape[0]
    NF = n_exp + 1
    P = 128
    T = 2 * P
    NU = n_tok // T
    CH = hid // P
    tail = dim - P
    TURNS = [0, n_exp, 1, 2, 3]
    LAYERS = [n_exp, 0, 1, 2, 3]
    assert n_exp == 4 and n_tok % T == 0 and CH % 2 == 0
    b1_e, b2_e = experts[1], experts[3]
    w1s = [experts[0][e] for e in range(n_exp)] + [mlp[0]]
    w2s = [experts[2][e] for e in range(n_exp)] + [mlp[2]]
    b1s = [b1_e[e] for e in range(n_exp)] + [mlp[1]]
    b2s = [b2_e[e] for e in range(n_exp)] + [mlp[3]]

    with ExitStack() as ctx:
        def sb(label, shape, dt):
            return ctx.enter_context(nc.sbuf_tensor(f"f_{label}", shape, dt))

        def ps(label, shape, dt=F32):
            return ctx.enter_context(nc.psum_tensor(f"f_{label}", shape, dt))

        def sem(label):
            return ctx.enter_context(nc.semaphore(f"f_{label}"))

        ident = sb("ident", [P, P], F32)
        lo_mask = sb("lo_mask", [P, 1], F32)
        row_mask = sb("row_mask", [P, 1], F32)
        ones = sb("ones", [P, P], F16)
        w1f = [sb(f"w1f{i}", [P, 2, hid], F32) for i in range(2)]
        w2f = [sb(f"w2f{i}", [P, CH, dim], F32) for i in range(2)]
        w1h = sb("w1h", [P, NF, 2, hid], F16)
        w1l = sb("w1l", [P, NF, 2, hid], F16)
        w2h = sb("w2h", [P, NF, CH, dim], F16)
        w2l = sb("w2l", [P, NF, CH, dim], F16)
        b1c = sb("b1c", [P, NF, CH], F32)
        b2f = sb("b2f", [P, NF, dim], F32)
        b2h = sb("b2h", [P, NF, dim], F16)
        b2r = sb("b2r", [P, NF, dim], F16)
        graw = sb("graw", [n_exp, 256], F32)
        gf = sb("gf", [P, 2, n_exp], F32)
        gh = sb("gh", [P, 2, n_exp], F16)
        gl = sb("gl", [P, 2, n_exp], F16)
        gb = sb("gb", [P, n_exp], F32)
        below = sb("below", [P, 2, n_exp, n_exp], F32)
        above = sb("above", [P, 2, n_exp, n_exp], F32)
        gcol = sb("gcol", [P, 2], F32)
        bcol = sb("bcol", [P, 2], F32)
        xin = [sb(f"xin{i}", [P, 2, 256], F32) for i in range(2)]
        hres = [sb(f"hres{i}", [P, 2, dim], F32) for i in range(2)]
        mh = sb("mh", [P, 2, T], F16)
        ml = sb("ml", [P, 2, T], F16)
        x4 = [sb(f"x4_{i}", [P, 2, dim], F32) for i in range(2)]
        stats = sb("stats", [P, 2, 6], F32)
        mv = sb("mv", [P, 2, 2], F32)
        rstd = sb("rstd", [P, 2], F32)
        eps = sb("eps", [P, 2], F32)
        minus_half = sb("minus_half", [P, 2], F32)
        spacer = sb("spacer", [P, 1], F32)
        xn = sb("xn", [P, 2, 256], F32)
        xf = sb("xf", [P, 2, T], F32)
        xh = [sb(f"xh{i}", [P, 2, T], F16) for i in range(2)]
        xl = [sb(f"xl{i}", [P, 2, T], F16) for i in range(2)]
        hf = [sb(f"hf{i}", [P, 2, T], F32) for i in range(3)]
        hh = [sb(f"hh{i}", [P, CH, T], F16) for i in range(2)]
        hl = [sb(f"hl{i}", [P, CH, T], F16) for i in range(2)]
        lg = sb("lg", [P, 2, n_exp], F32)
        ge = sb("ge", [P, 2, n_exp, n_exp], F32)
        gt = sb("gt", [P, 2, n_exp, n_exp], F32)
        rank = sb("rank", [P, 2, n_exp], F32)
        clg = sb("clg", [P, 2, n_exp], F32)
        csum = sb("csum", [P, 2, 1], F32)
        dlg = sb("dlg", [P, 2, n_exp], F32)
        th = sb("th", [P, 2, n_exp], F32)
        comb = [sb(f"comb{i}", [P, 2, n_exp], F32) for i in range(2)]
        acc = [sb(f"acc{i}", [P, 2, dim], F32) for i in range(2)]

        p1 = [ps(f"p1_{i}", [P, 512]) for i in range(3)]
        p2 = [ps(f"p2_{i}", [P, 512]) for i in range(2)]
        tx = ps("tx", [P, 512])
        tm = ps("tm", [P, 512])
        pg = ps("pg", [P, 512])

        consts = sem("consts")
        w_in = [sem(f"w_in{i}") for i in range(2)]
        small_in = sem("small_in")
        w_sc = sem("w_sc")
        w_hi = sem("w_hi")
        w_lo = sem("w_lo")
        g_t = sem("g_t")
        g_f = sem("g_f")
        x_in = sem("x_in")
        tx_s = sem("tx_s")
        mh_s = sem("mh_s")
        ml_s = sem("ml_s")
        p1_s = sem("p1_s")
        hf_s = sem("hf_s")
        hh_s = sem("hh_s")
        hl_s = sem("hl_s")
        p2_s = sem("p2_s")
        x4_s = sem("x4_s")
        acc0_s = sem("acc0_s")
        acc_s = sem("acc_s")
        st_s = sem("st_s")
        mv_s = sem("mv_s")
        rsqrt_s = sem("rsqrt_s")
        xn_s = sem("xn_s")
        tm_s = sem("tm_s")
        xf_s = sem("xf_s")
        xh_s = sem("xh_s")
        xl_s = sem("xl_s")
        pg_s = sem("pg_s")
        gate = sem("gate")
        th_s = sem("th_s")
        out_s = sem("out_s")
        GATE = 12

        LAG = {"B": 2, "A": 1, "E": 0, "F": -1}

        def steps(eng, body):
            def kinds(s):
                return {k for k, lag in LAG.items() if 0 <= s + lag < NU}
            first = 3
            n_pairs = (NU - 2 - first) // 2
            for s in range(-2, first):
                body(s, s % 2, kinds(s))
            if n_pairs > 0:
                with eng.Fori(0, n_pairs) as i:
                    body(2 * i + first, first % 2, set(LAG))
                    body(2 * i + first + 1, (first + 1) % 2, set(LAG))
            for s in range(first + 2 * max(n_pairs, 0), NU + 1):
                body(s, s % 2, kinds(s))

        def turns(s, kinds):
            return [(t, f) for t, f in enumerate(TURNS) if ("A" if f == n_exp else "E") in kinds]

        def turn_no(s, turn):
            if isinstance(s, int) and s < 0:
                return 0
            return 5 * s + turn + 1 - (1 if isinstance(s, int) and s == NU - 1 and turn > 1 else 0)

        def follows_itself(s, turn):
            return isinstance(s, int) and ((s, turn) in ((0, 0), (NU - 1, 2)))

        def mlp_inputs_read(s):
            return 0 if isinstance(s, int) and s < 0 else 3 * (turn_no(s - 1, 1) + 1)

        x_rows = x3.rearrange("(t p) d -> p t d", p=P)
        h_rows = h1.rearrange("(t p) d -> p t d", p=P)
        o_rows = out.rearrange("(t p) d -> p t d", p=P)
        block = ctx.enter_context(nc.Block())
        W_DMAS = 4
        n_small = 2 * NF + 2 + 1 + 2 * 3

        @block.sync
        def _(sp):
            def load_weights(n):
                f = LAYERS[n]
                if n >= 2:
                    sp.wait_ge(w_lo, 2 * (n - 1))
                sp.dma_start(w1f[n % 2][:, 0, :], w1s[f][0:P]).then_inc(w_in[n % 2], 16)
                for part in range(2):
                    sp.dma_start(w1f[n % 2][part * tail:(part + 1) * tail, 1, :], w1s[f][P:dim]).then_inc(w_in[n % 2], 16)
                sp.dma_start(w2f[n % 2][:], w2s[f].rearrange("(c p) e -> p c e", p=P)).then_inc(w_in[n % 2], 16)

            load_weights(0)
            sp.wait_ge(consts, 1)
            for f in range(NF):
                sp.dma_start(b1c[:, f, :], b1s[f].rearrange("(c p) -> p c", p=P), allow_slow_non_contiguous=True).then_inc(small_in, 16)
                sp.dma_start(b2f[0:2, f, :], b2s[f].partition_broadcast(2)).then_inc(small_in, 16)
            sp.dma_start(graw[:, 0:dim], gate_w).then_inc(small_in, 16)
            sp.dma_start(graw[:, dim:256], gate_w[:, P:dim]).then_inc(small_in, 16)
            sp.dma_start(gb[:], gate_b.partition_broadcast(P)).then_inc(small_in, 16)
            for col, vec in ((gcol, ln_g), (bcol, ln_b)):
                v = vec.rearrange("(p o) -> p o", o=1)
                sp.dma_start(col[:, 0:1], v[0:P]).then_inc(small_in, 16)
                for part in range(2):
                    sp.dma_start(col[part * tail:(part + 1) * tail, 1:2], v[P:dim]).then_inc(small_in, 16)
            load_weights(1)

            def step(s, par, kinds):
                if "B" in kinds:
                    u, b = s + 2, par
                    waits(sp,
                          (acc0_s, u - 1),
                          (tx_s, u))
                    sp.dma_start(xin[b][:, :, 0:dim], x_rows[:, bass.ds(u * 2, 2), :]).then_inc(x_in, 16)
                    sp.dma_start(xin[b][:, :, dim:256], x_rows[:, bass.ds(u * 2, 2), P:dim]).then_inc(x_in, 16)
                    sp.dma_start(hres[b][:], h_rows[:, bass.ds(u * 2, 2), :]).then_inc(x_in, 16)
                if isinstance(s, int) and s == -1:
                    for n in range(2, NF):
                        load_weights(n)
                if "F" in kinds:
                    u, b = s - 1, (par + 1) % 2
                    wait(sp, acc_s, 8 * (u + 1))
                    sp.dma_start(o_rows[:, bass.ds(u * 2, 2), :], acc[b][:]).then_inc(out_s, 16)

            steps(sp, step)
            sp.wait_ge(out_s, 16 * NU)

        @block.gpsimd
        def _(pool):
            pool.memset(b2f[:], 0.0).then_inc(consts, 1)
            pool.memset(ident[:], 0.0).then_inc(consts, 1)
            pool.memset(lo_mask[:], -1.0).then_inc(consts, 1)
            pool.memset(row_mask[:], 0.0).then_inc(consts, 1)
            pool.memset(ones[:], 1.0).then_inc(consts, 1)
            pool.memset(below[:], 0.0).then_inc(consts, 1)
            pool.memset(above[:], 0.0).then_inc(consts, 1)
            pool.memset(eps[:], EPS).then_inc(consts, 1)
            pool.memset(minus_half[:], -0.5).then_inc(consts, 1)
            pool.wait_ge(consts, 9)
            pool.memset(lo_mask[0:64, :], 0.0).then_inc(consts, 1)
            pool.wait_ge(consts, 10)
            pool.affine_select(out=ident[:], in_=ident[:], compare_op=ALU.not_equal, fill=1.0, base=0,
                               pattern=[[-1, P]], channel_multiplier=1).then_inc(consts, 1)
            pool.affine_select(out=row_mask[:], in_=row_mask[:], compare_op=ALU.not_equal, fill=-1.0, base=-1,
                               pattern=[[0, 1]], channel_multiplier=1).then_inc(consts, 1)
            pool.affine_select(out=below[:], in_=below[:], compare_op=ALU.is_ge, fill=1.0, base=0,
                               pattern=[[0, 2], [-1, n_exp], [1, n_exp]], channel_multiplier=0).then_inc(consts, 1)
            pool.affine_select(out=above[:], in_=above[:], compare_op=ALU.is_ge, fill=1.0, base=0,
                               pattern=[[0, 2], [1, n_exp], [-1, n_exp]], channel_multiplier=0).then_inc(consts, 1)

            def step(s, par, kinds):
                if "A" in kinds:
                    u, b = s + 1, (par + 1) % 2
                    wait(pool, x4_s, u + 1)
                    wait(pool, out_s, 16 * (u - 1))
                    pool.tensor_tensor(acc[b][:], x4[b][:], hres[b][:], ALU.add).then_inc(acc0_s, 1)
                    wait(pool, mv_s, 2 * (u + 1))
                    wait(pool, xn_s, 3 * u)
                    rsqrt(pool, rsqrt_s, u * RSQRT_OPS, mv[:, :, 1], rstd[:], eps[:], minus_half[:])

            steps(pool, step)

        @block.scalar
        def _(act):
            act.wait_ge(small_in, 16 * n_small)
            act.mul(b2f[:], b2f[:], WSCALE).then_inc(w_sc, 1)
            act.wait_ge(g_t, 1)
            act.mul(gf[:].rearrange("p a e -> p (a e)"), pg[:, 0:2 * n_exp], WSCALE).then_inc(g_f, 1)

            def high_parts(n):
                f = LAYERS[n]
                act.wait_ge(w_in[n % 2], 16 * W_DMAS * (n // 2 + 1))
                act.mul(w1h[:, f], w1f[n % 2][:], WSCALE).then_inc(w_hi, 1)
                act.mul(w2h[:, f], w2f[n % 2][:], WSCALE).then_inc(w_hi, 1)

            high_parts(0)

            def step(s, par, kinds):
                if "A" in kinds:
                    u = s + 1
                    wait(act, tx_s, u + 1)
                    wait(act, p1_s, mlp_inputs_read(s))
                    act.copy(mh[:].rearrange("p a t -> p (a t)"), tx[:, 0:2 * T]).then_inc(mh_s, 1)
                for turn, f in enumerate(TURNS):
                    if isinstance(s, int) and (s, turn) == (-1, 2):
                        high_parts(1)
                    if isinstance(s, int) and s == 0 and 0 < turn < NF - 1:
                        high_parts(turn + 1)
                    if turn == 2 and "E" in kinds:
                        wait(act, gate, GATE * s + 10)
                        act.activation(th[:], dlg[:], ACT.Tanh).then_inc(th_s, 1)
                    n = turn_no(s, turn)
                    for c in range(CH):
                        if turn == 4 and c == 2 and "A" in kinds:
                            u = s + 1
                            wait(act, tm_s, u + 1)
                            wait(act, xl_s, 2 * u)
                            for part in range(2):
                                act.activation(xf[:, part, :], tm[:, part * T:(part + 1) * T], ACT.Identity,
                                               scale=gcol[:, part:part + 1], bias=bcol[:, part:part + 1]).then_inc(xf_s, 1)
                        if (turn, f) in turns(s, kinds):
                            pair = c // 2
                            if c % 2 == 0:
                                wait(act, p1_s, 3 * n + pair + 1)
                                wait(act, hl_s, 3 * n + pair - 2)
                            act.activation(hf[pair][:, c % 2, :], p1[pair][:, (c % 2) * T:(c % 2) * T + T], ACT.Gelu,
                                           bias=b1c[:, f, c:c + 1], scale=1.0 / WSCALE).then_inc(hf_s, 1)

            steps(act, step)

        @block.vector
        def _(dve):
            dve.wait_ge(w_sc, 1)
            dve.tensor_copy(b2h[:], b2f[:]).then_inc(w_sc, 1)
            dve.wait_ge(consts, 14)
            dve.wait_ge(w_sc, 2)
            dve.scalar_tensor_tensor(out=b2r[:], in0=b2h[:], scalar=row_mask[:, 0:1], in1=b2f[:],
                                     op0=ALU.mult, op1=ALU.add).then_inc(g_f, 1)
            dve.wait_ge(g_f, 2)
            dve.tensor_copy(gh[:], gf[:]).then_inc(g_f, 1)
            dve.wait_ge(g_f, 3)
            dve.tensor_tensor(gl[:], gf[:], gh[:], ALU.subtract).then_inc(g_f, 1)

            def low_parts(n):
                f = LAYERS[n]
                for j, (wf, wh, wl) in enumerate(((w1f[n % 2], w1h, w1l), (w2f[n % 2], w2h, w2l))):
                    dve.wait_ge(w_hi, 2 * n + j + 1)
                    dve.scalar_tensor_tensor(out=wl[:, f], in0=wf[:], scalar=WSCALE, in1=wh[:, f],
                                             op0=ALU.mult, op1=ALU.subtract).then_inc(w_lo, 1)

            low_parts(0)

            def split_pairs(s, par, turn, pairs=range(CH // 2)):
                n, hb = turn_no(s, turn), (par + turn) % 2
                if isinstance(s, int) and s == 0 and 0 < turn < NF - 1 and pairs[0] == 0:
                    low_parts(turn + 1)
                for pair in pairs:
                    wait(dve, hf_s, CH * n + 2 * (pair + 1))
                    if pair == pairs[0]:
                        wait(dve, p2_s, 2 * (n if follows_itself(s, turn) else n - 1))
                    dve.tensor_copy(hh[hb][:, 2 * pair:2 * pair + 2, :], hf[pair][:]).then_inc(hh_s, 1)
                    wait(dve, hh_s, 3 * n + pair + 1)
                    dve.tensor_tensor(hl[hb][:, 2 * pair:2 * pair + 2, :], hf[pair][:], hh[hb][:, 2 * pair:2 * pair + 2, :],
                                      ALU.subtract).then_inc(hl_s, 1)

            def step(s, par, kinds):
                if "A" in kinds:
                    u = s + 1
                    wait(dve, mh_s, u + 1)
                    wait(dve, p1_s, mlp_inputs_read(s))
                    for part in range(2):
                        v = tx[:, part * T:(part + 1) * T]
                        if part == 0:
                            dve.tensor_tensor(ml[:, 0, :], v, mh[:, 0, :], ALU.subtract).then_inc(ml_s, 1)
                        else:
                            dve.scalar_tensor_tensor(out=ml[:, 1, :], in0=mh[:, 1, :], scalar=lo_mask[:, 0:1], in1=v,
                                                     op0=ALU.mult, op1=ALU.add).then_inc(ml_s, 1)
                if "E" in kinds:
                    split_pairs(s, par, 0)
                    rank_experts(s)
                if "F" in kinds:
                    add(s - 1, 3, (par + 1) % 2, (par + 1 + 4) % 2, turn_no(s - 1, 4))
                if "A" in kinds:
                    split_pairs(s, par, 1)
                if isinstance(s, int) and s == -1:
                    low_parts(1)
                if "E" in kinds:
                    weigh_experts(s, par)
                    wait(dve, acc0_s, s + 1)
                    add(s, 0, par, par, turn_no(s, 0))
                    split_pairs(s, par, 2)
                if "A" in kinds:
                    u, b = s + 1, (par + 1) % 2
                    wait(dve, p2_s, 2 * (turn_no(s, 1) + 1))
                    wait(dve, acc0_s, u - 1)
                    dve.scalar_tensor_tensor(out=x4[b][:], in0=p2[(par + 1) % 2][:, 0:2 * dim].rearrange("p (t d) -> p t d", t=2),
                                             scalar=1.0 / WSCALE, in1=xin[b][:, :, 0:dim],
                                             op0=ALU.mult, op1=ALU.add).then_inc(x4_s, 1)
                    wait(dve, x4_s, u + 1)
                    for t in range(2):
                        dve.bn_stats(stats[:, t, :], x4[b][:, t, :]).then_inc(st_s, 1)
                    wait(dve, rsqrt_s, RSQRT_OPS * u)
                    wait(dve, st_s, 2 * (u + 1))
                    dve.memset(spacer[:], 0.0)
                    for t in range(2):
                        dve.bn_aggr(mv[:, t, :], stats[:, t, :]).then_inc(mv_s, 1)
                if "E" in kinds:
                    split_pairs(s, par, 3, (0,))
                if "A" in kinds:
                    u, b = s + 1, (par + 1) % 2
                    wait(dve, rsqrt_s, RSQRT_OPS * (u + 1))
                    wait(dve, tm_s, u)
                    for t in range(2):
                        dve.tensor_scalar(xn[:, t, 0:dim], x4[b][:, t, :], mv[:, t, 0:1], rstd[:, t:t + 1],
                                          ALU.subtract, ALU.mult).then_inc(xn_s, 1)
                    wait(dve, xn_s, 3 * u + 2)
                    dve.tensor_copy(xn[:, :, dim:256], xn[:, :, P:dim]).then_inc(xn_s, 1)
                if "E" in kinds:
                    split_pairs(s, par, 3, (1, 2))
                    add(s, 1, par, par, turn_no(s, 2))
                    split_pairs(s, par, 4, (0,))
                if "A" in kinds:
                    u, b = s + 1, (par + 1) % 2
                    wait(dve, xf_s, 2 * (u + 1))
                    dve.tensor_copy(xh[b][:], xf[:]).then_inc(xh_s, 1)
                    wait(dve, xh_s, u + 1)
                    dve.tensor_tensor(xl[b][:, 0, :], xf[:, 0, :], xh[b][:, 0, :], ALU.subtract).then_inc(xl_s, 1)
                    dve.scalar_tensor_tensor(out=xl[b][:, 1, :], in0=xh[b][:, 1, :], scalar=lo_mask[:, 0:1], in1=xf[:, 1, :],
                                             op0=ALU.mult, op1=ALU.add).then_inc(xl_s, 1)
                if "E" in kinds:
                    split_pairs(s, par, 4, (1, 2))
                    add(s, 2, par, (par + 1) % 2, turn_no(s, 3))

            def add(u, e, b, bank, n):
                wait(dve, p2_s, 2 * (n + 1))
                for t in range(2):
                    wait(dve, acc_s, 8 * u + 2 * e)
                    dve.scalar_tensor_tensor(out=acc[b][:, t, :], in0=p2[bank][:, t * dim:(t + 1) * dim],
                                             scalar=comb[b][:, t, e:e + 1], in1=acc[b][:, t, :],
                                             op0=ALU.mult, op1=ALU.add).then_inc(acc_s, 1)

            def rank_experts(u):
                at = GATE * u
                rows = lg[:].unsqueeze(3).to_broadcast([P, 2, n_exp, n_exp])
                cols = lg[:].unsqueeze(2).to_broadcast([P, 2, n_exp, n_exp])
                wait(dve, pg_s, u + 1)
                dve.scalar_tensor_tensor(out=lg[:], in0=pg[:, 0:2 * n_exp].rearrange("p (t e) -> p t e", t=2), scalar=1.0 / WSCALE,
                                         in1=gb[:].unsqueeze(1).to_broadcast([P, 2, n_exp]), op0=ALU.mult, op1=ALU.add).then_inc(gate, 1)
                dve.wait_ge(gate, at + 1)
                dve.tensor_tensor(ge[:], cols, rows, ALU.is_ge).then_inc(gate, 1)
                dve.tensor_tensor(gt[:], cols, rows, ALU.is_gt).then_inc(gate, 1)
                dve.wait_ge(gate, at + 3)
                dve.tensor_tensor(ge[:], ge[:], below[:], ALU.mult).then_inc(gate, 1)
                dve.tensor_tensor(gt[:], gt[:], above[:], ALU.mult).then_inc(gate, 1)
                dve.wait_ge(gate, at + 5)
                dve.tensor_tensor(ge[:], ge[:], gt[:], ALU.add).then_inc(gate, 1)
                dve.wait_ge(gate, at + 6)
                dve.tensor_reduce(rank[:], ge[:], AX.X, ALU.add).then_inc(gate, 1)
                dve.wait_ge(gate, at + 7)
                dve.scalar_tensor_tensor(out=clg[:], in0=rank[:], scalar=2.0, in1=lg[:], op0=ALU.is_lt, op1=ALU.mult).then_inc(gate, 1)
                dve.wait_ge(gate, at + 8)
                dve.tensor_reduce(csum[:], clg[:], AX.X, ALU.add).then_inc(gate, 1)
                dve.wait_ge(gate, at + 9)
                dve.scalar_tensor_tensor(out=dlg[:], in0=csum[:].to_broadcast([P, 2, n_exp]), scalar=-0.5, in1=lg[:],
                                         op0=ALU.mult, op1=ALU.add).then_inc(gate, 1)

            def weigh_experts(u, par):
                at = GATE * u
                wait(dve, th_s, u + 1)
                dve.tensor_scalar(th[:], th[:], 0.5 / WSCALE, 0.5 / WSCALE, ALU.mult, ALU.add).then_inc(gate, 1)
                dve.wait_ge(gate, at + 11)
                wait(dve, acc_s, 8 * (u - 1))
                dve.scalar_tensor_tensor(out=comb[par][:], in0=rank[:], scalar=2.0, in1=th[:], op0=ALU.is_lt, op1=ALU.mult).then_inc(gate, 1)
                dve.wait_ge(gate, at + 12)

            steps(dve, step)

        @block.tensor
        def _(pe):
            pe.wait_ge(consts, 14)
            pe.wait_ge(small_in, 16 * n_small)
            for part in range(2):
                ins = pe.transpose(pg[:, part * n_exp:(part + 1) * n_exp], graw[:, part * P:(part + 1) * P], ident[0:n_exp, 0:n_exp])
            ins.then_inc(g_t, 1)
            pe.wait_ge(g_f, 4)
            pe.wait_ge(w_lo, 2)

            def first_product(n, f, c, src_h, src_l):
                pair = c // 2
                if c % 2 == 0:
                    wait(pe, hf_s, CH * (n - 1) + 2 * (pair + 1))
                cs = slice(c * P, (c + 1) * P)
                ins = products(pe, p1[pair][:, (c % 2) * T:(c % 2) * T + T],
                               [(w1h[:, f, 0, cs], src_h[:, 0, :]), (w1l[:, f, 0, cs], src_h[:, 0, :]), (w1h[:, f, 0, cs], src_l[:, 0, :]),
                                (w1h[:, f, 1, cs], src_l[:, 1, :]), (w1l[:, f, 1, cs], src_l[:, 1, :])])
                if c % 2 == 1:
                    ins.then_inc(p1_s, 1)

            def second_product(n, f, hb, bank, c, free):
                t, first = c // 3, 2 * (c % 3)
                if c == 0:
                    wait(pe, *free)
                wait(pe, hl_s, 3 * n + c % 3 + 1)
                for j in (first, first + 1):
                    ts = slice(t * P, (t + 1) * P)
                    o = p2[bank][:, t * dim:(t + 1) * dim]
                    pe.matmul(o, hh[hb][:, j, ts], w2h[:, f, j, :], start=(j == 0), stop=False)
                    pe.matmul(o, hh[hb][:, j, ts], w2l[:, f, j, :], start=False, stop=False)
                    pe.matmul(o, hl[hb][:, j, ts], w2h[:, f, j, :], start=False, stop=False)
                if c % 3 == 2:
                    pe.matmul(o, ones[:], b2r[:, f, :], start=False, stop=True).then_inc(p2_s, 1)

            def step(s, par, kinds):
                if "A" in kinds:
                    u, b = s + 1, (par + 1) % 2
                    wait(pe, ml_s, 2 * u)
                    wait(pe, x_in, 48 * (u + 1))
                    for part in range(2):
                        for t in range(2):
                            ins = pe.transpose(tx[:, part * T + t * P:part * T + (t + 1) * P], xin[b][:, t, part * P:(part + 1) * P], ident[:])
                    ins.then_inc(tx_s, 1)
                if "E" in kinds:
                    u = s
                    wait(pe, xl_s, 2 * (u + 1))
                    wait(pe, gate, GATE * (u - 1) + 1)
                    for t in range(2):
                        ts = slice(t * P, (t + 1) * P)
                        ins = products(pe, pg[:, t * n_exp:(t + 1) * n_exp],
                                       [(xh[par][:, 0, ts], gh[:, 0, :]), (xh[par][:, 0, ts], gl[:, 0, :]), (xl[par][:, 0, ts], gh[:, 0, :]),
                                        (xl[par][:, 1, ts], gh[:, 1, :]), (xl[par][:, 1, ts], gl[:, 1, :])])
                    ins.then_inc(pg_s, 1)
                for turn, f in enumerate(TURNS):
                    mine = ("A" if f == n_exp else "E") in kinds
                    pt, ps_, ppar, on = (turn - 1, s, par, "E") if turn else (4, s - 1, (par + 1) % 2, "F")
                    pf = TURNS[pt]
                    before = ("A" if pf == n_exp else on) in kinds
                    if before:
                        pn, phb = turn_no(ps_, pt), (ppar + pt) % 2
                        free = bank_free(ps_, pt)
                    if mine:
                        n = turn_no(s, turn)
                        if f == n_exp:
                            wait(pe, ml_s, 2 * (s + 2))
                            src_h, src_l = mh, ml
                        else:
                            src_h, src_l = xh[par], xl[par]
                        if isinstance(s, int) and s <= 0:
                            wait(pe, w_lo, 2 * (f + 2) if f < n_exp else 2)
                    for c in range(CH):
                        if mine:
                            first_product(n, f, c, src_h, src_l)
                        if before:
                            second_product(pn, pf, phb, phb, c, free)
                        if turn == 4 and c == 0 and "A" in kinds:
                            u = s + 1
                            wait(pe, xn_s, 3 * (u + 1))
                            wait(pe, xf_s, 2 * u)
                            for part in range(2):
                                for t in range(2):
                                    ins = pe.transpose(tm[:, part * T + t * P:part * T + (t + 1) * P], xn[:, t, part * P:(part + 1) * P], ident[:])
                            ins.then_inc(tm_s, 1)

            def bank_free(s, turn):
                if follows_itself(s, turn):
                    return (x4_s, 1) if turn == 0 else (acc_s, 8 * s + 2)
                if turn == 0:
                    return acc_s, 8 * (s - 1) + 6
                if turn == 1:
                    return acc_s, 8 * (s - 1) + 8
                if turn == 2:
                    return acc_s, 8 * s + 2
                if turn == 3:
                    if isinstance(s, int) and s == NU - 1:
                        return acc_s, 8 * s
                    return x4_s, s + 2
                return acc_s, 8 * s + 4

            steps(pe, step)


def vit_tower(nc, a, out):
    n_tok, dim = out.shape[0] * out.shape[1], out.shape[2]

    def scratch(label):
        return nc.dram_tensor(label, (n_tok, dim), F32, kind="Internal").ap()

    tokens, h1, x2, x3 = scratch("tokens"), scratch("h1"), scratch("x2"), scratch("x3")
    tokenize_phase(nc, a["x"], tokens, a["L0_tok_ln1_g"], a["L0_tok_ln1_b"], a["L0_tok_W"], a["L0_tok_b"],
                   a["L0_tok_ln2_g"], a["L0_tok_ln2_b"])
    attention_phase(nc, "a", tokens, h1, x2, a["L0_attn_w_qkv"], a["L0_attn_b_qkv"], a["L0_attn_w_proj"], a["L0_attn_b_proj"],
                    head_major=False, affine=None)
    attention_phase(nc, "b", x2, x3, None, a["L0_ffn_in_w"], a["L0_ffn_in_b"], a["L0_ffn_out_w"], a["L0_ffn_out_b"],
                    head_major=True, affine=(a["L0_ffn_ln1_g"], a["L0_ffn_ln1_b"]))
    ffn_phase(nc, x3, h1, out.rearrange("b n d -> (b n) d"),
              tuple(a["L0_ffn_mlp_" + k] for k in ("w1", "b1", "w2", "b2")),
              tuple(a["L0_ffn_exp_" + k] for k in ("w1", "b1", "w2", "b2")),
              a["L0_ffn_ln2_g"], a["L0_ffn_ln2_b"], a["L0_ffn_gate_w"], a["L0_ffn_gate_b"])


_OUTS = [((64, 196, 192), 'float32')]


def kernel(**inputs):
    import numpy as _np
    import concourse.bacc as _bacc
    from concourse import mybir as _mybir
    from concourse.bass_utils import run_bass_kernel_spmd as _run

    nc = _bacc.Bacc("TRN2", target_bir_lowering=False, num_devices=1)
    arrays, args = {}, {}
    for name in inputs:
        a = _np.ascontiguousarray(inputs[name])
        arrays[f"in_{name}_dram"] = a
        args[name] = nc.dram_tensor(f"in_{name}_dram", a.shape, _mybir.dt.from_np(a.dtype), kind="ExternalInput").ap()
    outs = [nc.dram_tensor(f"out_{i}_dram", shape, _mybir.dt.from_np(_np.dtype(dtype)), kind="ExternalOutput").ap()
            for i, (shape, dtype) in enumerate(_OUTS)]
    vit_tower(nc, args, outs[0])
    r = _run(nc, [arrays], core_ids=[0])
    return r.results[0]["out_0_dram"]
```
